# Optimizing a Trainium2 kernel written in Bass

```python
import numpy as np
import jax
import jax.numpy as jnp

def _softmax(x, axis=-1):
    return jax.nn.softmax(x, axis=axis)

def _gelu(x):
    return jax.nn.gelu(x, approximate=True)

def _silu(x):
    return jax.nn.silu(x)

def _sigmoid(x):
    return jax.nn.sigmoid(x)

def _layernorm(x, axis=-1, eps=1e-05):
    m = jnp.mean(x, axis=axis, keepdims=True)
    v = jnp.var(x, axis=axis, keepdims=True)
    return (x - m) / jnp.sqrt(v + eps)

def _scatter_add(tgt, idx, src, axis=0):
    return tgt.at[idx].add(src)

def _segment_sum(src, seg, n):
    return jax.ops.segment_sum(src, seg, n)
kernel_name = 'mk_macaron_d1_jaxref_r8_9c7f76'

def setup_inputs(seed: int=0):
    np.random.seed(seed)
    _w = jnp.asarray

    def _L0_attn_setup():
        import jax, jax.numpy as jnp
        import numpy as np
        D = 128
        B = 4
        S = 512
        LN_EPS = 1e-05

        def _layer_norm(x, gamma, beta):
            mu = jnp.mean(x, axis=-1, keepdims=True)
            var = jnp.mean(jnp.square(x - mu), axis=-1, keepdims=True)
            return (x - mu) * jax.lax.rsqrt(var + LN_EPS) * gamma + beta
        key = jax.random.key(seed)
        ks = jax.random.split(key, 5)
        scale = 1.0 / np.sqrt(D)
        return {'hidden_states': jax.random.normal(ks[0], (B, S, D), dtype=jnp.float32), 'attention_mask': jnp.ones((B, S), dtype=jnp.int32), 'Wk': jax.random.normal(ks[1], (D, D), dtype=jnp.float32) * scale, 'bk': jnp.zeros((D,), dtype=jnp.float32), 'Wka': jax.random.normal(ks[2], (D, D), dtype=jnp.float32) * scale, 'bka': jnp.zeros((D,), dtype=jnp.float32), 'Wv': jax.random.normal(ks[3], (D, D), dtype=jnp.float32) * scale, 'bv': jnp.zeros((D,), dtype=jnp.float32), 'gamma': jnp.ones((D,), dtype=jnp.float32), 'beta': jnp.zeros((D,), dtype=jnp.float32)}
    _L0_attn_in = _L0_attn_setup()

    def _L0_ffn_setup():
        import jax, jax.numpy as jnp
        import numpy as np
        D_IN, D_HID = (128, 512)

        def _ternary(key, shape):
            return jax.random.randint(key, shape, -1, 2).astype(jnp.float32)

        def _tlin(x, w, s):
            return jnp.einsum('bsi,oi->bso', x, w) * s
        key = jax.random.key(seed)
        ks = jax.random.split(key, 12)
        inv = lambda fan: 1.0 / np.sqrt(fan).astype(np.float32)
        return {'x': jax.random.normal(ks[0], (4, 256, D_IN), dtype=jnp.float32), 'w1_w': _ternary(ks[1], (D_HID, D_IN)), 'w1_s': jax.random.uniform(ks[2], (D_HID,), dtype=jnp.float32) * inv(D_IN), 'w2_w': _ternary(ks[3], (D_HID, D_IN)), 'w2_s': jax.random.uniform(ks[4], (D_HID,), dtype=jnp.float32) * inv(D_IN), 'h1_w': _ternary(ks[5], (D_HID, D_HID)), 'h1_s': jax.random.uniform(ks[6], (D_HID,), dtype=jnp.float32) * inv(D_HID), 'h2_w': _ternary(ks[7], (D_HID, D_HID)), 'h2_s': jax.random.uniform(ks[8], (D_HID,), dtype=jnp.float32) * inv(D_HID), 'w3_w': _ternary(ks[9], (D_IN, D_HID)), 'w3_s': jax.random.uniform(ks[10], (D_IN,), dtype=jnp.float32) * inv(D_HID)}
    _L0_ffn_in = _L0_ffn_setup()
    _d = {'L0_attn_hidden_states': _L0_attn_in['hidden_states'], 'L0_attn_attention_mask': _L0_attn_in['attention_mask'], 'L0_attn_Wk': _L0_attn_in['Wk'], 'L0_attn_bk': _L0_attn_in['bk'], 'L0_attn_Wka': _L0_attn_in['Wka'], 'L0_attn_bka': _L0_attn_in['bka'], 'L0_attn_Wv': _L0_attn_in['Wv'], 'L0_attn_bv': _L0_attn_in['bv'], 'L0_attn_gamma': _L0_attn_in['gamma'], 'L0_attn_beta': _L0_attn_in['beta'], 'L0_ffn_w1_w': _L0_ffn_in['w1_w'], 'L0_ffn_w1_s': _L0_ffn_in['w1_s'], 'L0_ffn_w2_w': _L0_ffn_in['w2_w'], 'L0_ffn_w2_s': _L0_ffn_in['w2_s'], 'L0_ffn_h1_w': _L0_ffn_in['h1_w'], 'L0_ffn_h1_s': _L0_ffn_in['h1_s'], 'L0_ffn_h2_w': _L0_ffn_in['h2_w'], 'L0_ffn_h2_s': _L0_ffn_in['h2_s'], 'L0_ffn_w3_w': _L0_ffn_in['w3_w'], 'L0_ffn_w3_s': _L0_ffn_in['w3_s']}
    _x0 = _d['L0_attn_hidden_states']
    _d['L0_attn_hidden_states'] = jax.random.normal(jax.random.fold_in(jax.random.key(seed), 1), (16, 256, 128), dtype=_x0.dtype)
    del _x0
    return _d

def reference(L0_attn_hidden_states, L0_attn_attention_mask, L0_attn_Wk, L0_attn_bk, L0_attn_Wka, L0_attn_bka, L0_attn_Wv, L0_attn_bv, L0_attn_gamma, L0_attn_beta, L0_ffn_w1_w, L0_ffn_w1_s, L0_ffn_w2_w, L0_ffn_w2_s, L0_ffn_h1_w, L0_ffn_h1_s, L0_ffn_h2_w, L0_ffn_h2_s, L0_ffn_w3_w, L0_ffn_w3_s):

    def _L0_attn_ref(hidden_states, attention_mask, Wk, bk, Wka, bka, Wv, bv, gamma, beta):
        import jax, jax.numpy as jnp
        import numpy as np
        D = 128
        B = 4
        S = 512
        LN_EPS = 1e-05

        def _layer_norm(x, gamma, beta):
            mu = jnp.mean(x, axis=-1, keepdims=True)
            var = jnp.mean(jnp.square(x - mu), axis=-1, keepdims=True)
            return (x - mu) * jax.lax.rsqrt(var + LN_EPS) * gamma + beta
        h = _layer_norm(hidden_states, gamma, beta)
        d_model = h.shape[-1]
        keys = jnp.einsum('bsd,ed->bse', h, Wk) + bk
        values = jnp.einsum('bsd,ed->bse', h, Wv) + bv
        key_att = jnp.einsum('bsd,ed->bse', keys, Wka) + bka
        keys_weight = jnp.exp(key_att / jnp.sqrt(jnp.asarray(d_model, h.dtype)))
        keys_weight = keys_weight / jnp.cumsum(keys_weight, axis=1)
        pooled_keys = jnp.cumsum(keys_weight * keys, axis=1)
        return pooled_keys * values

    def _L0_ffn_ref(x, w1_w, w1_s, w2_w, w2_s, h1_w, h1_s, h2_w, h2_s, w3_w, w3_s):
        import jax, jax.numpy as jnp
        import numpy as np
        D_IN, D_HID = (128, 512)

        def _ternary(key, shape):
            return jax.random.randint(key, shape, -1, 2).astype(jnp.float32)

        def _tlin(x, w, s):
            return jnp.einsum('bsi,oi->bso', x, w) * s
        h = jax.nn.silu(_tlin(x, w1_w, w1_s)) * _tlin(x, w2_w, w2_s)
        h = jax.nn.gelu(_tlin(h, h1_w, h1_s), approximate=False)
        h = jax.nn.gelu(_tlin(h, h2_w, h2_s), approximate=False)
        return _tlin(h, w3_w, w3_s)
    x = L0_attn_hidden_states
    x = x + 0.5 * _L0_ffn_ref(_layernorm(x, axis=-1), L0_ffn_w1_w, L0_ffn_w1_s, L0_ffn_w2_w, L0_ffn_w2_s, L0_ffn_h1_w, L0_ffn_h1_s, L0_ffn_h2_w, L0_ffn_h2_s, L0_ffn_w3_w, L0_ffn_w3_s)
    x = x + _L0_attn_ref(_layernorm(x, axis=-1), L0_attn_attention_mask, L0_attn_Wk, L0_attn_bk, L0_attn_Wka, L0_attn_bka, L0_attn_Wv, L0_attn_bv, L0_attn_gamma, L0_attn_beta)
    x = x + 0.5 * _L0_ffn_ref(_layernorm(x, axis=-1), L0_ffn_w1_w, L0_ffn_w1_s, L0_ffn_w2_w, L0_ffn_w2_s, L0_ffn_h1_w, L0_ffn_h1_s, L0_ffn_h2_w, L0_ffn_h2_s, L0_ffn_w3_w, L0_ffn_w3_s)
    return x

_drawn_inputs = setup_inputs


def setup_inputs(seed=0):
    import zlib

    import numpy as np

    out = dict(_drawn_inputs(seed))
    spreads = {'L0_attn_bk': (0.0, 0.1),
     'L0_attn_bka': (0.0, 0.1),
     'L0_attn_bv': (0.0, 0.1),
     'L0_attn_gamma': (1.0, 0.2),
     'L0_attn_beta': (0.0, 0.1)}
    factors = {}
    for name, (base, spread) in spreads.items():
        noise = np.random.default_rng([zlib.crc32(name.encode()), seed]).standard_normal(out[name].shape)
        drawn = base * np.exp(spread * noise) if base else spread * noise
        out[name] = jnp.asarray(drawn.astype(out[name].dtype))
    for name, factor in factors.items():
        out[name] = (out[name] * factor).astype(out[name].dtype)
    return out
```

```python
from contextlib import ExitStack

import concourse.bass as bass
from concourse import mybir

P = 128
F32 = mybir.dt.float32
F32R = mybir.dt.float32r
I32 = mybir.dt.int32
ALU = mybir.AluOpType
ACT = mybir.ActivationFunctionType
AX_X = mybir.AxisListType.X

TOK = 512
SUB = TOK // P
EPS = 1e-5

VEC = {"s1": (0, 4), "s2": (4, 4), "sh1": (8, 4), "sh2": (12, 4), "s3": (16, 1),
       "gamma": (17, 1), "beta": (18, 1), "bk": (19, 1), "bka": (20, 1), "bv": (21, 1)}
NVEC = 22


def macaron_block(nc, x, w1t, w2t, h1t, h2t, w3t, wkt, wkat, wvt, vecs, out, seq):
    ntok, D = x.shape
    HID = w1t.shape[1]
    MC = HID // P
    NT = ntok // TOK
    NB = ntok // P
    SCALE = float(D) ** -0.5
    assert D == P and TOK % seq == 0

    with ExitStack() as ctx:
        def sb(name, shape, dt=F32):
            return ctx.enter_context(nc.sbuf_tensor(name, shape, dt))

        def bank(name):
            return ctx.enter_context(nc.psum_tensor(name, [P, TOK], F32))

        def sem(name):
            return ctx.enter_context(nc.semaphore(name))

        x_sb = sb("x_sb", [P, NB * P])
        vec = sb("vec", [P, NVEC])
        names = {"w1": (1, HID), "w2": (1, HID), "h1": (MC, HID), "h2": (MC, HID), "w3": (MC, D)}
        raw = {n: sb(f"raw_{n}", [P, k * m]) for n, (k, m) in names.items()}
        whi = {n: sb(f"hi_{n}", [P, k * m], F32R) for n, (k, m) in names.items()}
        wlo = {n: sb(f"lo_{n}", [P, k * m], F32R) for n, (k, m) in names.items()}
        wk = sb("wk", [P, D])
        wka = sb("wka", [P, D])
        wv = sb("wv", [P, D])
        ident = sb("ident", [P, P])
        ones = sb("ones", [P, seq])
        half = sb("half", [P, SUB])
        s1_half = sb("s1_half", [P, MC])
        s12_half = sb("s12_half", [P, MC])
        s3_half = sb("s3_half", [P, 1])
        bka_s = sb("bka_s", [P, 1])
        lo_max = sb("lo_max", [P, len(names)])
        any_max = sb("any_max", [P, 1])
        inexact = sb("inexact", [P, 1])
        flag_i = sb("flag_i", [P, 1], I32)
        stats = sb("stats", [P, SUB, 6])
        mv = sb("mv", [P, SUB, 2])
        veps = sb("veps", [P, SUB])
        fence = sb("fence", [P, 1])
        rstd = sb("rstd", [P, SUB])
        z = sb("z", [P, TOK])
        xn_hi = sb("xn_hi", [P, TOK], F32R)
        xn_lo = sb("xn_lo", [P, TOK], F32R)
        tanh_b = [sb(f"tanh_{i}", [P, TOK]) for i in range(2)]
        gate_b = [sb(f"gate_{i}", [P, TOK]) for i in range(2)]
        full1 = [sb(f"full1_{i}", [P, TOK]) for i in range(2)]
        full23 = [sb(f"full23_{i}", [P, TOK]) for i in range(2)]
        act_hi = {n: sb(f"act{n}_hi", [P, MC, TOK], F32R) for n in (1, 2, 3)}
        act_lo = {n: sb(f"act{n}_lo", [P, MC, TOK], F32R) for n in (1, 2, 3)}
        delta = sb("delta", [P, TOK])
        h_t = sb("h_t", [P, TOK])
        keys = sb("keys", [P, TOK])
        kw = sb("kw", [P, TOK])
        csum = sb("csum", [P, TOK])
        rcsum = sb("rcsum", [P, TOK])
        wgt = sb("wgt", [P, TOK])
        wgt_keys = sb("wgt_keys", [P, TOK])
        pooled = sb("pooled", [P, TOK])

        gate_ps = [bank(f"gate_ps{i}") for i in range(2)]
        up_ps = [bank(f"up_ps{i}") for i in range(2)]
        hid_ps = [bank(f"hid_ps{i}") for i in range(2)]
        y_ps = bank("y_ps")
        xt_ps = bank("xt_ps")
        key_ps, att_ps, val_ps = gate_ps[0], gate_ps[1], up_ps[0]

        s_x0, s_xr, s_vec, s_wa, s_wh1, s_wh2, s_w3, s_watt, s_out = (
            sem(n) for n in ("s_x0", "s_xr", "s_vec", "s_wa", "s_wh1", "s_wh2", "s_w3", "s_watt", "s_out"))
        s_const = sem("s_const")
        s_small = sem("s_small")
        s_whi = sem("s_whi")
        s_wlo = sem("s_wlo")
        s_max = sem("s_max")
        s_inexact = sem("s_inexact")
        s_fps = sem("s_fps")
        s_bn, s_mv, s_ve, s_pow, s_z = (sem(n) for n in ("s_bn", "s_mv", "s_ve", "s_pow", "s_z"))
        s_t, s_xhi, s_xlo = (sem(n) for n in ("s_t", "s_xhi", "s_xlo"))
        s_p1, s_tanh, s_gate, s_full1 = (sem(n) for n in ("s_p1", "s_tanh", "s_gate", "s_full1"))
        s_p = {n: sem(f"s_p{n}") for n in (2, 3)}
        s_gelu = {n: sem(f"s_gelu{n}") for n in (2, 3)}
        s_hi = {n: sem(f"s_hi{n}") for n in (1, 2, 3)}
        s_lo = {n: sem(f"s_lo{n}") for n in (1, 2, 3)}
        s_p4, s_delta, s_dt, s_add = (sem(n) for n in ("s_p4", "s_delta", "s_dt", "s_add"))
        s_at, s_ht, s_key, s_keysb, s_att, s_kw, s_val = (
            sem(n) for n in ("s_at", "s_ht", "s_key", "s_keysb", "s_att", "s_kw", "s_val"))
        s_cs, s_rc, s_wg, s_wgk, s_pool, s_adelta = (
            sem(n) for n in ("s_cs", "s_rc", "s_wg", "s_wgk", "s_pool", "s_adelta"))

        def col(name, m=0):
            return vec[:, VEC[name][0] + m:VEC[name][0] + m + 1]

        def wblk(parts, name, k, m):
            n = names[name][1]
            return parts[name][:, k * n + m * P:k * n + (m + 1) * P]

        def xblk(t, j):
            return x_sb[:, bass.ds(t * TOK + j * P, P)]

        block = ctx.enter_context(nc.Block())

        @block.sync
        def _(eng):
            def xload(t0, t1, s):
                src = x[t0 * TOK:t1 * TOK, :].rearrange("(b p) d -> p b d", p=P)
                dst = x_sb[:, t0 * TOK:t1 * TOK].rearrange("p (b d) -> p b d", d=P)
                eng.dma_start(dst, src).then_inc(s, 16)

            def wload(dst, src, s):
                k = src.shape[0] // P
                eng.dma_start(dst[:, :].rearrange("p (k n) -> p k n", k=k),
                              src.rearrange("(k p) n -> p k n", p=P)).then_inc(s, 16)

            xload(0, 1, s_x0)
            wload(raw["w1"], w1t, s_wa)
            wload(raw["w2"], w2t, s_wa)
            wload(raw["h1"], h1t, s_wh1)
            xload(1, NT, s_xr)
            wload(raw["h2"], h2t, s_wh2)
            wload(raw["w3"], w3t, s_w3)
            for dst, src in ((wk, wkt), (wka, wkat), (wv, wvt)):
                wload(dst, src, s_watt)
            with eng.Fori(0, NT) as t:
                eng.wait_ge(s_add, t + (2 * NT + 2))
                dst = out[bass.ds(t * TOK, TOK), :].rearrange("(b p) d -> p b d", p=P)
                src = x_sb[:, bass.ds(t * TOK, TOK)].rearrange("p (b d) -> p b d", d=P)
                eng.dma_start(dst, src).then_inc(s_out, 16)
            eng.wait_ge(s_out, 16 * NT)

        @block.gpsimd
        def _(eng):
            eng.memset(ident[:, :], 0.0).then_inc(s_const, 1)
            eng.memset(ones[:, :], 1.0).then_inc(s_const, 1)
            eng.memset(half[:, :], -0.5).then_inc(s_const, 1)
            eng.wait_ge(s_const, 3)
            eng.affine_select(out=ident[:, :], in_=ident[:, :], compare_op=ALU.not_equal, fill=1.0,
                              base=0, pattern=[[-1, P]], channel_multiplier=1).then_inc(s_const, 1)
            with eng.Fori(0, 3 * NT) as n:
                eng.wait_ge(s_ve, n + 1)
                eng.tensor_tensor(rstd[:, :], veps[:, :], half[:, :], ALU.pow).then_inc(s_pow, 1)

        def run(eng, body, base):
            body(-1, base)
            body(0, base)
            with eng.Fori(1, NT - 1) as i:
                body(i, base, steady=True)
            body(NT - 1, base)
            body(NT, base)

        def active(i, lag, steady):
            return steady or 0 <= i + lag < NT

        @block.tensor
        def _(eng):
            def products(ps, parts, done, general):
                seq_ = []
                for name, k, m, hi, lo in parts:
                    if general:
                        seq_ += [(wblk(wlo, name, k, m), lo), (wblk(wlo, name, k, m), hi)]
                    seq_ += [(wblk(whi, name, k, m), lo), (wblk(whi, name, k, m), hi)]
                for n, (w, a) in enumerate(seq_):
                    mm = eng.matmul(ps, w, a, start=(n == 0), stop=(n == len(seq_) - 1))
                if done is not None:
                    mm.then_inc(done, 1)

            def transpose4(dst, src, done):
                for j in range(SUB):
                    mm = eng.transpose(dst[:, j * P:(j + 1) * P], src[:, j * P:(j + 1) * P], ident[:, :])
                mm.then_inc(done, 1)

            def t_in(T, free):
                eng.wait_ge(s_z, T + 1)
                free()
                transpose4(xt_ps, z, s_t)

            def p1(T, m, general):
                c = MC * T + m
                if m == 0:
                    eng.wait_ge(s_xlo, T + 1)
                if not (isinstance(T, int) and c < 2):
                    eng.wait_ge(s_full1, c - 1)
                products(gate_ps[m % 2][:, :], [("w1", 0, m, xn_hi[:, :], xn_lo[:, :])], None, general)
                products(up_ps[m % 2][:, :], [("w2", 0, m, xn_hi[:, :], xn_lo[:, :])], s_p1, general)

            def p23(n, T, m, general):
                prev, w = (1, "h1") if n == 2 else (2, "h2")
                if m == 0:
                    eng.wait_ge(s_lo[prev], MC * T + MC)
                if n == 2 and m < 2:
                    if not (isinstance(T, int) and T == 0):
                        eng.wait_ge(s_gelu[3], MC * T - MC + m + 3)
                elif n == 3 and m < 2:
                    eng.wait_ge(s_gelu[2], MC * T + m + 3)
                else:
                    eng.wait_ge(s_gelu[n], MC * T + m - 1)
                products(hid_ps[m % 2][:, :],
                         [(w, k, m, act_hi[prev][:, k, :], act_lo[prev][:, k, :]) for k in range(MC)],
                         s_p[n], general)

            def p4(T, reads, general):
                eng.wait_ge(s_lo[3], MC * T + MC)
                eng.wait_ge(s_add, reads)
                products(y_ps[:, :], [("w3", k, 0, act_hi[3][:, k, :], act_lo[3][:, k, :])
                                      for k in range(MC)], s_p4, general)

            def d_t(T):
                eng.wait_ge(s_delta, T + 1)
                transpose4(y_ps, delta, s_dt)

            def ffn_step(general):
                def body(i, f, steady=False):
                    on = lambda lag: active(i, lag, steady)
                    T = i + f * NT
                    LT = i + 2 * f * NT
                    A = T + f * NT
                    if on(0):
                        p23(2, T, 0, general)
                    if on(-1):
                        p4(T - 1, A, general)
                    if on(0):
                        p23(2, T, 1, general)
                    if on(1):
                        if not isinstance(i, int) or i > -1:
                            t_in(LT + 1, lambda: eng.wait_ge(s_xlo, T + 1))
                        elif f == 0:
                            t_in(LT + 1, lambda: None)
                        else:
                            t_in(LT + 1, lambda: eng.wait_ge(s_ht, NT))
                    if on(0):
                        p23(2, T, 2, general)
                    if on(-1):
                        d_t(T - 1)
                    if on(0):
                        p23(2, T, 3, general)
                    if on(1):
                        p1(T + 1, 0, general)
                        p1(T + 1, 1, general)
                    if on(0):
                        p23(3, T, 0, general)
                    if on(1):
                        p1(T + 1, 2, general)
                    if on(0):
                        p23(3, T, 1, general)
                    if on(1):
                        p1(T + 1, 3, general)
                    if on(0):
                        p23(3, T, 2, general)
                        p23(3, T, 3, general)
                return body

            def att_step(i, _, steady=False):
                on = lambda lag: active(i, lag, steady)
                if on(0):
                    eng.wait_ge(s_ht, i + 1)
                    eng.matmul(key_ps[:, :], wk[:, :], h_t[:, :], start=True, stop=True).then_inc(s_key, 1)
                    eng.wait_ge(s_keysb, i + 1)
                    eng.matmul(att_ps[:, :], wka[:, :], keys[:, :], start=True, stop=True).then_inc(s_att, 1)
                    if not isinstance(i, int) or i > 0:
                        eng.wait_ge(s_adelta, i)
                    eng.matmul(val_ps[:, :], wv[:, :], h_t[:, :], start=True, stop=True).then_inc(s_val, 1)
                if on(-1):
                    eng.wait_ge(s_adelta, i)
                    eng.wait_ge(s_add, i + NT)
                    transpose4(y_ps, delta, s_at)
                if on(1):
                    t_in(i + (NT + 1), (lambda: eng.wait_ge(s_ht, i + 1)) if not isinstance(i, int) or i > -1
                         else (lambda: eng.wait_ge(s_xlo, NT)))

            eng.wait_ge(s_const, 4)
            eng.wait_ge(s_inexact, 1)
            eng.matmul(y_ps[0:1, 0:1], inexact[:, 0:1], ones[:, 0:1], start=True, stop=True).then_inc(s_fps, 1)
            eng.wait_ge(s_whi, len(names))
            eng.wait_ge(s_wlo, len(names))
            eng.wait_ge(s_watt, 48)
            with eng.register("flag") as flag:
                eng.wait_ge(s_add, 1)
                eng.reg_load(flag, flag_i[0:1, 0:1])

                def everything(general):
                    run(eng, ffn_step(general), 0)
                    run(eng, att_step, 0)
                    run(eng, ffn_step(general), 1)

                with eng.If_ne(flag, 0):
                    everything(True)
                with eng.Else():
                    everything(False)

        @block.scalar
        def _(eng):
            eng.dma_start(vec[:, :], vecs).then_inc(s_vec, 16)

            for n, s, v in (("w1", s_wa, 32), ("w2", s_wa, 32), ("h1", s_wh1, 16), ("h2", s_wh2, 16), ("w3", s_w3, 16)):
                eng.wait_ge(s, v)
                eng.activation(whi[n][:, :], raw[n][:, :], ACT.Copy).then_inc(s_whi, 1)
            eng.wait_ge(s_vec, 16)
            eng.wait_ge(s_small, 4)

            def xn_high(T, LT):
                eng.wait_ge(s_t, LT + 1)
                eng.activation(xn_hi[:, :], xt_ps[:, :], ACT.Copy).then_inc(s_xhi, 1)

            def tanh(T, m):
                c = MC * T + m
                eng.wait_ge(s_p1, c + 1)
                if not (isinstance(T, int) and c < 2):
                    eng.wait_ge(s_gate, c - 1)
                eng.activation(tanh_b[m % 2][:, :], gate_ps[m % 2][:, :], ACT.Tanh,
                               scale=s1_half[:, m:m + 1]).then_inc(s_tanh, 1)

            def high1(T, m):
                eng.wait_ge(s_full1, MC * T + m + 1)
                eng.activation(act_hi[1][:, m, :], full1[m % 2][:, :], ACT.Copy).then_inc(s_hi[1], 1)

            def gelu_high(n, T, m):
                eng.wait_ge(s_p[n], MC * T + m + 1)
                if n == 2 and m < 2:
                    if not (isinstance(T, int) and T == 0):
                        eng.wait_ge(s_lo[3], MC * T - MC + m + 3)
                elif n == 3 and m < 2:
                    eng.wait_ge(s_lo[2], MC * T + m + 3)
                else:
                    eng.wait_ge(s_lo[n], MC * T + m - 1)
                eng.activation(full23[m % 2][:, :], hid_ps[m % 2][:, :], ACT.Gelu,
                               scale=col("sh1" if n == 2 else "sh2", m)).then_inc(s_gelu[n], 1)
                eng.wait_ge(s_gelu[n], MC * T + m + 1)
                eng.activation(act_hi[n][:, m, :], full23[m % 2][:, :], ACT.Copy).then_inc(s_hi[n], 1)

            def ffn_step(i, f, steady=False):
                on = lambda lag: active(i, lag, steady)
                T = i + f * NT
                if on(0):
                    gelu_high(2, T, 0)
                if on(-1):
                    eng.wait_ge(s_p4, T)
                    eng.activation(delta[:, :], y_ps[:, :], ACT.Copy, scale=s3_half[:, 0:1]).then_inc(s_delta, 1)
                if on(0):
                    gelu_high(2, T, 1)
                if on(1):
                    xn_high(T + 1, i + 2 * f * NT + 1)
                if on(0):
                    gelu_high(2, T, 2)
                    gelu_high(2, T, 3)
                if on(1):
                    tanh(T + 1, 0)
                    tanh(T + 1, 1)
                    high1(T + 1, 0)
                if on(0):
                    gelu_high(3, T, 0)
                if on(1):
                    tanh(T + 1, 2)
                    high1(T + 1, 1)
                if on(0):
                    gelu_high(3, T, 1)
                if on(1):
                    tanh(T + 1, 3)
                    high1(T + 1, 2)
                if on(0):
                    gelu_high(3, T, 2)
                if on(1):
                    high1(T + 1, 3)
                if on(0):
                    gelu_high(3, T, 3)

            def att_step(i, _, steady=False):
                on = lambda lag: active(i, lag, steady)
                if on(0):
                    eng.wait_ge(s_key, i + 1)
                    if not isinstance(i, int) or i > 0:
                        eng.wait_ge(s_wgk, i)
                    eng.activation(keys[:, :], key_ps[:, :], ACT.Identity, bias=col("bk")).then_inc(s_keysb, 1)
                    eng.wait_ge(s_att, i + 1)
                    if not isinstance(i, int) or i > 0:
                        eng.wait_ge(s_wg, i)
                    eng.activation(kw[:, :], att_ps[:, :], ACT.Exp, bias=bka_s[:, 0:1], scale=SCALE).then_inc(s_kw, 1)
                if on(1):
                    eng.wait_ge(s_t, i + (NT + 2))
                    eng.activation(h_t[:, :], xt_ps[:, :], ACT.Identity, bias=col("beta"),
                                   scale=col("gamma")).then_inc(s_ht, 1)

            run(eng, ffn_step, 0)
            run(eng, att_step, 0)
            run(eng, ffn_step, 1)

        @block.vector
        def _(eng):
            eng.wait_ge(s_vec, 16)
            eng.tensor_scalar(s1_half[:, :], vec[:, 0:MC], 0.5, None, ALU.mult).then_inc(s_small, 1)
            eng.tensor_scalar(s3_half[:, :], col("s3"), 0.5, None, ALU.mult).then_inc(s_small, 1)
            eng.tensor_scalar(bka_s[:, :], col("bka"), SCALE, None, ALU.mult).then_inc(s_small, 1)
            eng.wait_ge(s_small, 3)
            eng.tensor_tensor(s12_half[:, :], s1_half[:, :], vec[:, 4:4 + MC], ALU.mult).then_inc(s_small, 1)

            for q, n in enumerate(names):
                eng.wait_ge(s_whi, q + 1)
                eng.tensor_tensor(wlo[n][:, :], raw[n][:, :], whi[n][:, :].bitcast(F32),
                                  ALU.subtract).then_inc(s_wlo, 1)
                eng.wait_ge(s_wlo, q + 1)
                eng.tensor_reduce(lo_max[:, q:q + 1], wlo[n][:, :].bitcast(F32), AX_X, ALU.max,
                                  apply_absolute_value=True).then_inc(s_max, 1)
            eng.wait_ge(s_max, len(names))
            eng.tensor_reduce(any_max[:, :], lo_max[:, :], AX_X, ALU.max).then_inc(s_max, 1)
            eng.wait_ge(s_max, len(names) + 1)
            eng.tensor_scalar(inexact[:, :], any_max[:, :], 0.0, None, ALU.is_gt).then_inc(s_inexact, 1)
            eng.wait_ge(s_fps, 1)
            eng.tensor_copy(flag_i[0:1, 0:1], y_ps[0:1, 0:1]).then_inc(s_add, 1)

            def norm(n, t, a, b):
                for j in range(SUB):
                    eng.bn_stats(stats[:, j, :], xblk(t, j)).then_inc(s_bn, 1)
                eng.wait_ge(s_bn, SUB * n + SUB)
                eng.memset(fence[:, :], 0.0)
                for j in range(SUB):
                    eng.bn_aggr(mv[:, j, :], stats[:, j, :]).then_inc(s_mv, 1)
                eng.wait_ge(s_mv, SUB * n + SUB)
                eng.tensor_scalar(veps[:, :], mv[:, :, 1], a, b, ALU.mult, ALU.add).then_inc(s_ve, 1)
                eng.wait_ge(s_pow, n + 1)
                if not isinstance(n, int) or n > 0:
                    eng.wait_ge(s_t, n)
                for j in range(SUB):
                    zz = eng.tensor_scalar(z[:, j * P:(j + 1) * P], xblk(t, j), mv[:, j, 0:1], rstd[:, j:j + 1],
                                           ALU.subtract, ALU.mult)
                zz.then_inc(s_z, 1)

            def gate_up(T, m):
                c = MC * T + m
                eng.wait_ge(s_tanh, c + 1)
                eng.scalar_tensor_tensor(gate_b[m % 2][:, :], tanh_b[m % 2][:, :], 1.0, gate_ps[m % 2][:, :],
                                         ALU.add, ALU.mult).then_inc(s_gate, 1)
                eng.wait_ge(s_gate, c + 1)
                if not (isinstance(T, int) and c < 2):
                    eng.wait_ge(s_hi[1], c - 1)
                eng.scalar_tensor_tensor(full1[m % 2][:, :], up_ps[m % 2][:, :], s12_half[:, m:m + 1],
                                         gate_b[m % 2][:, :], ALU.mult, ALU.mult).then_inc(s_full1, 1)

            def low(n, T, m):
                eng.wait_ge(s_hi[n], MC * T + m + 1)
                full = full1 if n == 1 else full23
                eng.tensor_tensor(act_lo[n][:, m, :], full[m % 2][:, :], act_hi[n][:, m, :].bitcast(F32),
                                  ALU.subtract).then_inc(s_lo[n], 1)

            def add_delta(t, ready, n):
                eng.wait_ge(ready, n)
                eng.tensor_tensor(x_sb[:, bass.ds(t * TOK, TOK)], x_sb[:, bass.ds(t * TOK, TOK)], y_ps[:, :],
                                  ALU.add).then_inc(s_add, 1)

            def ffn_step(i, f, steady=False):
                on = lambda lag: active(i, lag, steady)
                T = i + f * NT
                if on(1):
                    if f == 0 and isinstance(i, int):
                        if i == -1:
                            eng.wait_ge(s_x0, 16)
                        if i == 0:
                            eng.wait_ge(s_xr, 16)
                    if f == 1 and isinstance(i, int) and i == -1:
                        eng.wait_ge(s_add, 2 * NT + 1)
                    norm(i + 2 * f * NT + 1, i + 1, 1.0, EPS)
                if on(0):
                    low(2, T, 0)
                    low(2, T, 1)
                if on(1):
                    eng.wait_ge(s_xhi, T + 2)
                    eng.tensor_tensor(xn_lo[:, :], xt_ps[:, :], xn_hi[:, :].bitcast(F32),
                                      ALU.subtract).then_inc(s_xlo, 1)
                if on(0):
                    low(2, T, 2)
                if on(-1):
                    add_delta(i - 1, s_dt, T)
                if on(0):
                    low(2, T, 3)
                if on(1):
                    gate_up(T + 1, 0)
                    gate_up(T + 1, 1)
                    low(1, T + 1, 0)
                if on(0):
                    low(3, T, 0)
                if on(1):
                    gate_up(T + 1, 2)
                    low(1, T + 1, 1)
                if on(0):
                    low(3, T, 1)
                if on(1):
                    gate_up(T + 1, 3)
                    low(1, T + 1, 2)
                if on(0):
                    low(3, T, 2)
                if on(1):
                    low(1, T + 1, 3)
                if on(0):
                    low(3, T, 3)

            def att_step(i, _, steady=False):
                on = lambda lag: active(i, lag, steady)
                if on(1):
                    if isinstance(i, int) and i == -1:
                        eng.wait_ge(s_add, NT + 1)
                    norm(i + (NT + 1), i + 1, 1.0 + EPS, EPS * EPS)
                if on(0):
                    eng.wait_ge(s_kw, i + 1)
                    for b in range(TOK // seq):
                        cs = eng.tensor_tensor_scan(csum[:, b * seq:(b + 1) * seq], ones[:, :],
                                                    kw[:, b * seq:(b + 1) * seq], 0.0, ALU.mult, ALU.add)
                    cs.then_inc(s_cs, 1)
                if on(-1):
                    add_delta(i - 1, s_at, i)
                if on(0):
                    eng.wait_ge(s_cs, i + 1)
                    eng.reciprocal(rcsum[:, :], csum[:, :]).then_inc(s_rc, 1)
                    eng.wait_ge(s_rc, i + 1)
                    eng.tensor_tensor(wgt[:, :], kw[:, :], rcsum[:, :], ALU.mult).then_inc(s_wg, 1)
                    eng.wait_ge(s_wg, i + 1)
                    eng.tensor_tensor(wgt_keys[:, :], wgt[:, :], keys[:, :], ALU.mult).then_inc(s_wgk, 1)
                    eng.wait_ge(s_wgk, i + 1)
                    for b in range(TOK // seq):
                        pl = eng.tensor_tensor_scan(pooled[:, b * seq:(b + 1) * seq], ones[:, :],
                                                    wgt_keys[:, b * seq:(b + 1) * seq], 0.0, ALU.mult, ALU.add)
                    pl.then_inc(s_pool, 1)
                    eng.wait_ge(s_pool, i + 1)
                    eng.wait_ge(s_val, i + 1)
                    if not isinstance(i, int) or i > 0:
                        eng.wait_ge(s_at, i)
                    eng.scalar_tensor_tensor(delta[:, :], val_ps[:, :], col("bv"), pooled[:, :],
                                             ALU.add, ALU.mult).then_inc(s_adelta, 1)

            run(eng, ffn_step, 0)
            run(eng, att_step, 0)
            run(eng, ffn_step, 1)


def kernel(**inputs):
    import numpy as _np
    import concourse.bacc as _bacc
    from concourse import mybir as _mybir
    from concourse.bass_utils import run_bass_kernel_spmd as _run

    def get(n):
        return _np.asarray(inputs[n])

    X = get("L0_attn_hidden_states")
    nb, seq, D = X.shape
    arrays = {"x": _np.ascontiguousarray(X.reshape(nb * seq, D))}
    for n, src in (("w1t", "L0_ffn_w1_w"), ("w2t", "L0_ffn_w2_w"), ("h1t", "L0_ffn_h1_w"), ("h2t", "L0_ffn_h2_w"),
                   ("w3t", "L0_ffn_w3_w"), ("wkt", "L0_attn_Wk"), ("wkat", "L0_attn_Wka"), ("wvt", "L0_attn_Wv")):
        arrays[n] = _np.ascontiguousarray(get(src).T)
    cols = [get(f"L0_ffn_{n}_s").reshape(-1, P).T for n in ("w1", "w2", "h1", "h2", "w3")]
    cols += [get(f"L0_attn_{n}").reshape(1, P).T for n in ("gamma", "beta", "bk", "bka", "bv")]
    arrays["vecs"] = _np.ascontiguousarray(_np.concatenate(cols, axis=1))

    nc = _bacc.Bacc("TRN2", target_bir_lowering=False, num_devices=1)
    args = [nc.dram_tensor(n, a.shape, _mybir.dt.from_np(a.dtype), kind="ExternalInput").ap()
            for n, a in arrays.items()]
    out = nc.dram_tensor("out", (nb * seq, D), F32, kind="ExternalOutput").ap()
    macaron_block(nc, *args, out, seq)
    r = _run(nc, [arrays], core_ids=[0])
    return r.results[0]["out"].reshape(nb, seq, D)
```

```python
from contextlib import ExitStack

import concourse.bass as bass
from concourse import mybir

P = 128
F32 = mybir.dt.float32
F32R = mybir.dt.float32r
I32 = mybir.dt.int32
ALU = mybir.AluOpType
ACT = mybir.ActivationFunctionType
AX_X = mybir.AxisListType.X

TOK = 512
SUB = TOK // P
ACT_Z = 2
EPS = 1e-5

VEC = {"s1": (0, 4), "s2": (4, 4), "sh1": (8, 4), "sh2": (12, 4), "s3": (16, 1),
       "gamma": (17, 1), "beta": (18, 1), "bk": (19, 1), "bka": (20, 1), "bv": (21, 1)}
NVEC = 22

START = {
    "PE": (
        "",
        "t p1.0 p1.1 p1.2 p1.3",
    ),
    "ACT": (
        "zwait hi:h1 z abs:w2",
        "t hi:h2 abs:w1 p1.0 hi:w3 p1.1 h1.0 abs:h2 p1.2 h1.1 abs:h1 p1.3 abs:w3 zwait h1.2 h1.3 z",
    ),
    "DVE": (
        "stats norm hi:w1 hi:w2",
        "lo:w2 lo:w1 t lo:h2 p1.0 stats p1.1 l1.0 lo:w3 p1.2 l1.1 p1.3 norm l1.2 l1.3",
    ),
}
ORDER = {
    "PE": (
        "p2.0 p2.1 t p2.2 p1.0 p2.3 a:t p1.1 p4 p1.2 p1.3 a:keys p3.0 p3.1 dt a:logits p3.2 p3.3",
        "t p2.0 p2.1 p2.2 p1.0 a:values p1.1 p2.3 p4 p1.2 p1.3 dt b:t p3.0 p3.1 a:dt p3.2 b:keys p3.3",
        "b:logits p2.0 p2.1 t p2.2 p2.3 p1.0 p1.1 p4 b:values p1.2 p1.3 dt p3.0 p3.1 b:dt p3.2 p3.3",
        "p2.0 p2.1 t p2.2 p1.0 p2.3 p1.1 p4 p1.2 p3.0 p1.3 p3.1 p3.2 p3.3 dt",
    ),
    "ACT": (
        "p2.0 t p2.1 a:zwait p2.2 a:z p1.0 p2.3 zwait p1.1 z h1.0 a:t h1.1 p1.2 p1.3 a:keys p4 h1.2 p3.0 "
        "h1.3 p3.1 a:logits p3.2 p3.3",
        "p2.0 t p2.1 b:zwait p2.2 p1.0 p1.1 b:z p2.3 h1.0 p4 p1.2 h1.1 p1.3 b:t p3.0 h1.2 p3.1 p3.2 h1.3 "
        "b:keys p3.3 zwait b:logits z",
        "p2.0 p2.1 t p2.2 p1.0 p2.3 p1.1 h1.0 p4 p1.2 h1.1 p1.3 h1.2 p3.0 h1.3 p3.1 p3.2 zwait p3.3 z",
        "p2.0 t p2.1 p2.2 p1.0 p2.3 p1.1 zwait p4 p1.2 h1.0 h1.1 p3.0 p1.3 h1.2 p3.1 h1.3 p3.2 p3.3 z",
    ),
    "DVE": (
        "a:stats p2.0 t a:norm stats p2.1 p2.2 p1.0 p1.1 norm p2.3 l1.0 p1.2 l1.1 p1.3 l1.2 l1.3 dt p3.0 "
        "b:stats p3.1 a:cumsum a:recip.0 p3.2 a:recip.1 p3.3",
        "t p2.0 a:weight p2.1 a:weight_keys p2.2 a:pool p1.0 b:norm p1.1 l1.0 a:values p2.3 p1.2 dt l1.1 "
        "p1.3 p3.0 a:dt stats p3.1 l1.2 p3.2 l1.3 p3.3 norm b:cumsum",
        "b:recip.0 b:recip.1 p2.0 b:weight t b:weight_keys p2.1 b:pool p2.2 p1.0 p1.1 b:values p2.3 l1.0 "
        "l1.1 p1.2 dt p1.3 b:dt p3.0 stats l1.2 l1.3 p3.1 norm p3.2 p3.3",
        "p2.0 t stats p2.1 p2.2 p1.0 p2.3 p1.1 l1.0 l1.1 p1.2 p3.0 p1.3 l1.2 l1.3 p3.1 norm p3.2 dt p3.3",
    ),
}
POOL_LOW = ("h1",)
AHEAD = {"stats": 2, "norm": 2, "zwait": 2, "z": 2, "p1": 1, "h1": 1, "l1": 1, "t": 1, "p4": -1, "dt": -1}


def macaron_block(nc, x, w1t, w2t, h1t, h2t, w3t, wkt, wkat, wvt, vecs, out, seq):
    ntok, D = x.shape
    HID = w1t.shape[1]
    MC = HID // P
    NT = ntok // TOK
    NB = ntok // P
    SCALE = float(D) ** -0.5
    assert D == P and TOK % seq == 0

    with ExitStack() as ctx:
        def sb(name, shape, dt=F32):
            return ctx.enter_context(nc.sbuf_tensor(name, shape, dt))

        def bank(name):
            return ctx.enter_context(nc.psum_tensor(name, [P, TOK], F32))

        def sem(name):
            return ctx.enter_context(nc.semaphore(name))

        x_sb = sb("x_sb", [P, 2 * NB * P])
        vec = sb("vec", [P, NVEC])
        names = {"w1": (1, HID), "w2": (1, HID), "h1": (MC, HID), "h2": (MC, HID), "w3": (MC, D)}
        raw = {n: sb(f"raw_{n}", [P, k * m]) for n, (k, m) in names.items()}
        whi = {n: sb(f"hi_{n}", [P, k * m], F32R) for n, (k, m) in names.items()}
        wlo = {n: sb(f"lo_{n}", [P, k * m], F32R) for n, (k, m) in names.items()}
        wk = sb("wk", [P, D])
        wka = sb("wka", [P, D])
        wv = sb("wv", [P, D])
        ident = sb("ident", [P, P])
        ones = sb("ones", [P, seq])
        half = sb("half", [P, SUB])
        s1_half = sb("s1_half", [P, MC])
        s12_half = sb("s12_half", [P, MC])
        s3_half = sb("s3_half", [P, 1])
        bka_s = sb("bka_s", [P, 1])
        lo_abs = sb("lo_abs", [P, MC * HID])
        lo_sum = sb("lo_sum", [P, len(names)])
        lo_sums = sb("lo_sums", [P, 1])
        inexact = sb("inexact", [P, 1])
        flag_i = sb("flag_i", [P, 1], I32)
        stats = sb("stats", [P, SUB, 6])
        mv = sb("mv", [P, SUB, 2])
        veps = sb("veps", [P, SUB])
        fence = sb("fence", [P, 1])
        neg_mean = sb("neg_mean", [P, SUB])
        rstd = sb("rstd", [P, SUB])
        nmr = sb("nmr", [P, SUB])
        z = sb("z", [P, TOK])
        xn_hi = sb("xn_hi", [P, TOK], F32R)
        xn_lo = sb("xn_lo", [P, TOK], F32R)
        tanh_b = [sb(f"tanh_{i}", [P, TOK]) for i in range(2)]
        gate_b = [sb(f"gate_{i}", [P, TOK]) for i in range(2)]
        full1 = [sb(f"full1_{i}", [P, TOK]) for i in range(2)]
        full23 = [sb(f"full23_{i}", [P, TOK]) for i in range(2)]
        act_hi = {n: sb(f"act{n}_hi", [P, MC, TOK], F32R) for n in (1, 2, 3)}
        act_lo = {n: sb(f"act{n}_lo", [P, MC, TOK], F32R) for n in (1, 2, 3)}
        delta = sb("delta", [P, TOK])
        adelta = sb("adelta", [P, TOK])
        h_t = sb("h_t", [P, TOK])
        keys = sb("keys", [P, TOK])
        kw = sb("kw", [P, TOK])
        csum = sb("csum", [P, TOK])
        rcsum = sb("rcsum", [P, TOK])
        wgt = sb("wgt", [P, TOK])
        wgt_keys = sb("wgt_keys", [P, TOK])
        pooled = sb("pooled", [P, TOK])

        gate_ps = [bank(f"gate_ps{i}") for i in range(2)]
        up_ps = [bank(f"up_ps{i}") for i in range(2)]
        hid_ps = [bank(f"hid_ps{i}") for i in range(2)]
        y_ps = bank("y_ps")
        xt_ps = bank("xt_ps")

        s_x0, s_xr, s_vec, s_w1, s_w2, s_wh1, s_wh2, s_w3, s_watt, s_out = (
            sem(n) for n in ("s_x0", "s_xr", "s_vec", "s_w1", "s_w2", "s_wh1", "s_wh2", "s_w3", "s_watt", "s_out"))
        s_const = sem("s_const")
        s_small = sem("s_small")
        s_whi = {n: sem(f"s_whi_{n}") for n in names}
        s_wlo = {n: sem(f"s_wlo_{n}") for n in names}
        s_wabs = sem("s_wabs")
        s_wsum = sem("s_wsum")
        s_inexact = sem("s_inexact")
        s_bn, s_mv, s_ve, s_pow, s_z, s_t = (sem(n) for n in ("s_bn", "s_mv", "s_ve", "s_pow", "s_z", "s_t"))
        s_nmr, s_za = sem("s_nmr"), sem("s_za")
        s_xhi, s_xlo = sem("s_xhi"), sem("s_xlo")
        s_fps = sem("s_fps")
        s_flag = sem("s_flag")
        s_p1, s_tanh, s_gate, s_full1 = (sem(n) for n in ("s_p1", "s_tanh", "s_gate", "s_full1"))
        s_p = {n: sem(f"s_p{n}") for n in (2, 3)}
        s_gelu = {n: sem(f"s_gelu{n}") for n in (2, 3)}
        s_hi = {n: sem(f"s_hi{n}") for n in (1, 2, 3)}
        s_lo = {n: sem(f"s_lo{n}") for n in (1, 2, 3)}
        s_p4, s_delta, s_dt, s_x1 = (sem(n) for n in ("s_p4", "s_delta", "s_dt", "s_x1"))
        s_ht, s_key, s_keysb, s_att, s_kw, s_val = (
            sem(n) for n in ("s_ht", "s_key", "s_keysb", "s_att", "s_kw", "s_val"))
        s_cs, s_rc, s_wg, s_wgk, s_pool, s_adelta, s_at, s_x2 = (
            sem(n) for n in ("s_cs", "s_rc", "s_wg", "s_wgk", "s_pool", "s_adelta", "s_at", "s_x2"))

        order = list(names)
        w_loaded = {"w1": (s_w1, 16), "w2": (s_w2, 16), "h1": (s_wh1, 16), "h2": (s_wh2, 16), "w3": (s_w3, 16)}

        def col(name, m=0):
            return vec[:, VEC[name][0] + m:VEC[name][0] + m + 1]

        def wblk(parts, name, k, m):
            n = names[name][1]
            return parts[name][:, k * n + m * P:k * n + (m + 1) * P]

        def xblk(t, j):
            return x_sb[:, bass.ds(t * TOK + j * P, P)]

        block = ctx.enter_context(nc.Block())

        @block.sync
        def _(eng):
            def xload(t0, t1, s):
                src = x[t0 * TOK:t1 * TOK, :].rearrange("(b p) d -> p b d", p=P)
                dst = x_sb[:, t0 * TOK:t1 * TOK].rearrange("p (b d) -> p b d", d=P)
                eng.dma_start(dst, src).then_inc(s, 16)

            def wload(dst, src, s):
                k = src.shape[0] // P
                eng.dma_start(dst[:, :].rearrange("p (k n) -> p k n", k=k),
                              src.rearrange("(k p) n -> p k n", p=P)).then_inc(s, 16)

            xload(0, 1, s_x0)
            wload(raw["w1"], w1t, s_w1)
            wload(raw["w2"], w2t, s_w2)
            wload(raw["h1"], h1t, s_wh1)
            wload(raw["h2"], h2t, s_wh2)
            wload(raw["w3"], w3t, s_w3)
            xload(1, NT, s_xr)
            for dst, src in ((wk, wkt), (wka, wkat), (wv, wvt)):
                wload(dst, src, s_watt)
            with eng.Fori(0, NT) as t:
                eng.wait_ge(s_x1, t + (NT + 1))
                dst = out[bass.ds(t * TOK, TOK), :].rearrange("(b p) d -> p b d", p=P)
                src = x_sb[:, bass.ds(t * TOK + NT * TOK, TOK)].rearrange("p (b d) -> p b d", d=P)
                eng.dma_start(dst, src).then_inc(s_out, 16)
            eng.wait_ge(s_out, 16 * NT)

        @block.gpsimd
        def _(eng):
            for s in (s_adelta, s_x2, s_wgk, s_za):
                eng.sem_inc(s, 1)
            eng.memset(ident[:, :], 0.0).then_inc(s_const, 1)
            eng.memset(ones[:, :], 1.0).then_inc(s_const, 1)
            eng.memset(half[:, :], -0.5).then_inc(s_const, 1)
            eng.wait_ge(s_const, 3)
            eng.affine_select(out=ident[:, :], in_=ident[:, :], compare_op=ALU.not_equal, fill=1.0,
                              base=0, pattern=[[-1, P]], channel_multiplier=1).then_inc(s_const, 1)

            def norm(n):
                eng.wait_ge(s_ve, n + 1)
                eng.wait_ge(s_za, n + 1)
                eng.tensor_tensor(rstd[:, :], veps[:, :], half[:, :], ALU.pow).then_inc(s_pow, 1)
                eng.wait_ge(s_pow, n + 1)
                eng.tensor_tensor(nmr[:, :], neg_mean[:, :], rstd[:, :], ALU.mult).then_inc(s_nmr, 1)

            norm(0)
            for n in POOL_LOW:
                eng.wait_ge(s_whi[n], 1)
                eng.tensor_tensor(wlo[n][:, :], raw[n][:, :], whi[n][:, :].bitcast(F32),
                                  ALU.subtract).then_inc(s_wlo[n], 1)
            with eng.Fori(1, 3 * NT) as n:
                norm(n)

        GROUP, ATT = 3, 2
        FIRST = 2
        LOOPS = NT // ATT
        assert FIRST + GROUP * LOOPS + 2 == 2 * NT

        def schedule(engine, emit, start):
            def step(i, order, L):
                for item in order.split():
                    which, _, stage = item.rpartition(":")
                    stage, _, chunk = stage.partition(".")
                    chunk = int(chunk) if chunk else None
                    if which in ("hi", "lo", "abs"):
                        emit(which, None, stage, L)
                    elif which and L is not None:
                        emit("att_" + stage, chunk, ATT * L + "ab".index(which), L)
                    elif not which:
                        t = i + AHEAD.get(stage, 0)
                        if not isinstance(t, int) or 0 <= t < 2 * NT:
                            emit(stage, chunk, t, L)

            eng, orders = {"PE": nc.tensor, "ACT": nc.scalar, "DVE": nc.vector}[engine], ORDER[engine]
            if start:
                step(-2, START[engine][0], None)
                step(-1, START[engine][1], None)
                return
            for i in range(0, FIRST):
                step(i, orders[GROUP], None)
            with eng.Fori(0, LOOPS) as L:
                for s in range(GROUP):
                    step(GROUP * L + (FIRST + s), orders[s], L)
            for i in range(2 * NT - 2, 2 * NT + 1):
                step(i, orders[GROUP], None)

        class Uses:
            def __init__(self, start, per_loop):
                self.n, self.per_loop, self.loop_base = start, per_loop, None

            def peek(self, L):
                if L is not None and self.loop_base is None:
                    self.loop_base = self.n
                if L is None and self.loop_base is not None:
                    assert self.n == self.loop_base + self.per_loop
                    self.n, self.loop_base = self.n + (LOOPS - 1) * self.per_loop, None
                return self.n if L is None else L * self.per_loop + self.n

            def next(self, L):
                n = self.peek(L)
                self.n += 1
                return n

        @block.tensor
        def _(eng):
            def products(ps, parts, done, general):
                seq_ = []
                for name, k, m, hi, lo in parts:
                    if general:
                        seq_ += [(wblk(wlo, name, k, m), lo), (wblk(wlo, name, k, m), hi)]
                    seq_ += [(wblk(whi, name, k, m), lo), (wblk(whi, name, k, m), hi)]
                for n, (w, a) in enumerate(seq_):
                    mm = eng.matmul(ps, w, a, start=(n == 0), stop=(n == len(seq_) - 1))
                if done is not None:
                    mm.then_inc(done, 1)

            def transpose4(dst, src, done):
                for j in range(SUB):
                    mm = eng.transpose(dst[:, j * P:(j + 1) * P], src[:, j * P:(j + 1) * P], ident[:, :])
                mm.then_inc(done, 1)

            def p1(T, m, general):
                c = MC * T + m
                if m == 0:
                    eng.wait_ge(s_xlo, T + 1)
                    if isinstance(T, int) and T == 0:
                        for n in ("w1", "w2"):
                            eng.wait_ge(s_whi[n], 1)
                            eng.wait_ge(s_wlo[n], 1)
                if not (isinstance(T, int) and c < 2):
                    eng.wait_ge(s_full1, c - 1)
                products(gate_ps[m % 2][:, :], [("w1", 0, m, xn_hi[:, :], xn_lo[:, :])], None, general)
                products(up_ps[m % 2][:, :], [("w2", 0, m, xn_hi[:, :], xn_lo[:, :])], s_p1, general)

            def p23(n, T, m, general):
                prev, w = (1, "h1") if n == 2 else (2, "h2")
                if m == 0:
                    eng.wait_ge(s_lo[prev], MC * T + MC)
                if n == 2 and m < 2:
                    if not (isinstance(T, int) and T == 0):
                        eng.wait_ge(s_gelu[3], MC * T - MC + m + 3)
                elif n == 3 and m < 2:
                    eng.wait_ge(s_gelu[2], MC * T + m + 3)
                else:
                    eng.wait_ge(s_gelu[n], MC * T + m - 1)
                products(hid_ps[m % 2][:, :],
                         [(w, k, m, act_hi[prev][:, k, :], act_lo[prev][:, k, :]) for k in range(MC)],
                         s_p[n], general)

            def stages(general, transposed, xt_reader):
                norms = Uses(transposed, GROUP + ATT)
                last = {"xt": xt_reader, "y": [(s_flag, 1)], "inside": False}

                def free(bank, reader):
                    for s, n in last[bank]:
                        eng.wait_ge(s, n)
                    last[bank] = [reader]

                def emit(stage, chunk, t, L):
                    if L is not None and not last["inside"]:
                        last.update(xt=[(s_xlo, GROUP * L + FIRST), (s_adelta, ATT * L + 1)],
                                    y=[(s_x1, GROUP * L + (FIRST - 1)), (s_x2, ATT * L + 1)], inside=True)
                    if L is None and last["inside"]:
                        last.update(xt=[(s_xlo, 2 * NT - 1), (s_adelta, NT + 1)],
                                    y=[(s_x1, 2 * NT - 3), (s_x2, NT + 1)], inside=False)
                    if stage == "p1":
                        p1(t, chunk, general)
                    elif stage in ("p2", "p3"):
                        p23(int(stage[1]), t, chunk, general)
                    elif stage in ("t", "att_t"):
                        n = norms.next(L)
                        if ACT_Z < SUB:
                            eng.wait_ge(s_z, n + 1)
                        eng.wait_ge(s_za, n + 2)
                        free("xt", (s_xlo if stage == "t" else s_ht, t + 1))
                        transpose4(xt_ps, z, s_t)
                    elif stage == "p4":
                        eng.wait_ge(s_lo[3], MC * t + MC)
                        free("y", (s_delta, t + 1))
                        products(y_ps[:, :], [("w3", k, 0, act_hi[3][:, k, :], act_lo[3][:, k, :])
                                              for k in range(MC)], s_p4, general)
                    elif stage == "dt":
                        free("y", (s_x1, t + 1))
                        transpose4(y_ps, delta, s_dt)
                    elif stage == "att_keys":
                        free("xt", (s_keysb, t + 1))
                        eng.wait_ge(s_watt, 48)
                        eng.matmul(xt_ps[:, :], wk[:, :], h_t[:, :], start=True, stop=True).then_inc(s_key, 1)
                    elif stage == "att_logits":
                        free("xt", (s_kw, t + 1))
                        eng.matmul(xt_ps[:, :], wka[:, :], keys[:, :], start=True, stop=True).then_inc(s_att, 1)
                    elif stage == "att_values":
                        free("xt", (s_adelta, t + 2))
                        eng.matmul(xt_ps[:, :], wv[:, :], h_t[:, :], start=True, stop=True).then_inc(s_val, 1)
                    elif stage == "att_dt":
                        eng.wait_ge(s_adelta, t + 2)
                        free("y", (s_x2, t + 2))
                        transpose4(y_ps, adelta, s_at)
                return emit

            eng.wait_ge(s_const, 4)
            schedule("PE", stages(True, 0, []), True)
            eng.wait_ge(s_inexact, 1)
            eng.matmul(y_ps[0:1, 0:1], inexact[:, 0:1], ones[:, 0:1], start=True, stop=True).then_inc(s_fps, 1)
            with eng.register("flag") as flag:
                eng.wait_ge(s_flag, 1)
                eng.reg_load(flag, flag_i[0:1, 0:1])
                with eng.If_ne(flag, 0):
                    schedule("PE", stages(True, 1, [(s_xlo, 1)]), False)
                with eng.Else():
                    schedule("PE", stages(False, 1, [(s_xlo, 1)]), False)

        @block.scalar
        def _(eng):
            eng.dma_start(vec[:, :], vecs).then_inc(s_vec, 16)

            abs_order = [i[4:] for i in " ".join(START["ACT"]).split() if i.startswith("abs:")]

            def weight(what, n):
                if what == "hi":
                    eng.wait_ge(*w_loaded[n])
                    eng.activation(whi[n][:, :], raw[n][:, :], ACT.Copy).then_inc(s_whi[n], 1)
                else:
                    q = abs_order.index(n)
                    eng.wait_ge(s_wlo[n], 1)
                    if q > 0:
                        eng.wait_ge(s_wabs, q)
                    eng.activation(lo_abs[:, 0:wlo[n].shape[1]], wlo[n][:, :].bitcast(F32), ACT.Abs,
                                   accum_out=lo_sum[:, q:q + 1]).then_inc(s_wabs, 1)

            eng.wait_ge(s_vec, 16)
            eng.wait_ge(s_small, 4)

            def tanh(T, m):
                c = MC * T + m
                eng.wait_ge(s_p1, c + 1)
                if not (isinstance(T, int) and c < 2):
                    eng.wait_ge(s_gate, c - 1)
                eng.activation(tanh_b[m % 2][:, :], gate_ps[m % 2][:, :], ACT.Tanh,
                               scale=s1_half[:, m:m + 1]).then_inc(s_tanh, 1)

            def high1(T, m):
                eng.wait_ge(s_full1, MC * T + m + 1)
                eng.activation(act_hi[1][:, m, :], full1[m % 2][:, :], ACT.Copy).then_inc(s_hi[1], 1)

            def gelu_high(n, T, m):
                eng.wait_ge(s_p[n], MC * T + m + 1)
                if n == 2 and m < 2:
                    if not (isinstance(T, int) and T == 0):
                        eng.wait_ge(s_lo[3], MC * T - MC + m + 3)
                elif n == 3 and m < 2:
                    eng.wait_ge(s_lo[2], MC * T + m + 3)
                else:
                    eng.wait_ge(s_lo[n], MC * T + m - 1)
                eng.activation(full23[m % 2][:, :], hid_ps[m % 2][:, :], ACT.Gelu,
                               scale=col("sh1" if n == 2 else "sh2", m)).then_inc(s_gelu[n], 1)
                eng.wait_ge(s_gelu[n], MC * T + m + 1)
                eng.activation(act_hi[n][:, m, :], full23[m % 2][:, :], ACT.Copy).then_inc(s_hi[n], 1)

            def z_blocks(t):
                for j in range(ACT_Z):
                    zz = eng.activation(z[:, j * P:(j + 1) * P], xblk(t, j), ACT.Identity, bias=nmr[:, j:j + 1],
                                        scale=rstd[:, j:j + 1])
                zz.then_inc(s_za, 1)

            norms, z_norms = Uses(0, GROUP + ATT), Uses(0, GROUP + ATT)

            def emit(stage, chunk, t, L):
                if stage in ("hi", "abs"):
                    weight(stage, t)
                elif stage == "p1":
                    tanh(t, chunk)
                elif stage == "h1":
                    high1(t, chunk)
                elif stage in ("zwait", "att_zwait"):
                    n = z_norms.next(L)
                    eng.wait_ge(s_nmr, n + 1)
                    if not isinstance(n, int) or n > 0:
                        eng.wait_ge(s_t, n)
                elif stage in ("z", "att_z"):
                    z_blocks(t)
                elif stage in ("p2", "p3"):
                    gelu_high(int(stage[1]), t, chunk)
                elif stage == "p4":
                    eng.wait_ge(s_p4, t + 1)
                    eng.activation(delta[:, :], y_ps[:, :], ACT.Copy, scale=s3_half[:, 0:1]).then_inc(s_delta, 1)
                elif stage == "t":
                    eng.wait_ge(s_t, norms.next(L) + 1)
                    eng.activation(xn_hi[:, :], xt_ps[:, :], ACT.Copy).then_inc(s_xhi, 1)
                elif stage == "att_t":
                    eng.wait_ge(s_t, norms.next(L) + 1)
                    eng.activation(h_t[:, :], xt_ps[:, :], ACT.Identity, bias=col("beta"),
                                   scale=col("gamma")).then_inc(s_ht, 1)
                elif stage == "att_keys":
                    eng.wait_ge(s_key, t + 1)
                    eng.wait_ge(s_wgk, t + 1)
                    eng.activation(keys[:, :], xt_ps[:, :], ACT.Identity, bias=col("bk")).then_inc(s_keysb, 1)
                elif stage == "att_logits":
                    eng.wait_ge(s_att, t + 1)
                    eng.activation(kw[:, :], xt_ps[:, :], ACT.Exp, bias=bka_s[:, 0:1],
                                   scale=SCALE).then_inc(s_kw, 1)

            schedule("ACT", emit, True)
            schedule("ACT", emit, False)

        @block.vector
        def _(eng):
            eng.wait_ge(s_vec, 16)
            eng.tensor_scalar(s1_half[:, :], vec[:, 0:MC], 0.5, None, ALU.mult).then_inc(s_small, 1)
            eng.tensor_scalar(s3_half[:, :], col("s3"), 0.5, None, ALU.mult).then_inc(s_small, 1)
            eng.tensor_scalar(bka_s[:, :], col("bka"), SCALE, None, ALU.mult).then_inc(s_small, 1)
            eng.wait_ge(s_small, 3)
            eng.tensor_tensor(s12_half[:, :], s1_half[:, :], vec[:, 4:4 + MC], ALU.mult).then_inc(s_small, 1)

            def weight(what, n):
                if what == "hi":
                    eng.wait_ge(*w_loaded[n])
                    eng.tensor_copy(whi[n][:, :], raw[n][:, :]).then_inc(s_whi[n], 1)
                else:
                    eng.wait_ge(*w_loaded[n])
                    eng.wait_ge(s_whi[n], 1)
                    eng.tensor_tensor(wlo[n][:, :], raw[n][:, :], whi[n][:, :].bitcast(F32),
                                      ALU.subtract).then_inc(s_wlo[n], 1)

            def norm_stats(n, t, a, b):
                for j in range(SUB):
                    eng.bn_stats(stats[:, j, :], xblk(t, j)).then_inc(s_bn, 1)
                eng.wait_ge(s_bn, SUB * n + SUB)
                eng.memset(fence[:, :], 0.0)
                for j in range(SUB):
                    eng.bn_aggr(mv[:, j, :], stats[:, j, :]).then_inc(s_mv, 1)
                eng.wait_ge(s_mv, SUB * n + SUB)
                eng.tensor_scalar(neg_mean[:, :], mv[:, :, 0], -1.0, None, ALU.mult)
                eng.tensor_scalar(veps[:, :], mv[:, :, 1], a, b, ALU.mult, ALU.add).then_inc(s_ve, 1)

            def norm_apply(n, t):
                if ACT_Z == SUB:
                    return
                eng.wait_ge(s_nmr, n + 1)
                if not isinstance(n, int) or n > 0:
                    eng.wait_ge(s_t, n)
                for j in range(ACT_Z, SUB):
                    zz = eng.tensor_scalar(z[:, j * P:(j + 1) * P], xblk(t, j), mv[:, j, 0:1], rstd[:, j:j + 1],
                                           ALU.subtract, ALU.mult)
                zz.then_inc(s_z, 1)

            def gate_up(T, m):
                c = MC * T + m
                eng.wait_ge(s_tanh, c + 1)
                eng.scalar_tensor_tensor(gate_b[m % 2][:, :], tanh_b[m % 2][:, :], 1.0, gate_ps[m % 2][:, :],
                                         ALU.add, ALU.mult).then_inc(s_gate, 1)
                eng.wait_ge(s_gate, c + 1)
                if not (isinstance(T, int) and c < 2):
                    eng.wait_ge(s_hi[1], c - 1)
                eng.scalar_tensor_tensor(full1[m % 2][:, :], up_ps[m % 2][:, :], s12_half[:, m:m + 1],
                                         gate_b[m % 2][:, :], ALU.mult, ALU.mult).then_inc(s_full1, 1)

            def low(n, T, m):
                eng.wait_ge(s_hi[n], MC * T + m + 1)
                full = full1 if n == 1 else full23
                eng.tensor_tensor(act_lo[n][:, m, :], full[m % 2][:, :], act_hi[n][:, m, :].bitcast(F32),
                                  ALU.subtract).then_inc(s_lo[n], 1)

            def batches():
                return [slice(b * seq, (b + 1) * seq) for b in range(TOK // seq)]

            norms_a, norms_b, x2_adds = Uses(0, GROUP + ATT), Uses(0, GROUP + ATT), Uses(0, ATT)

            def emit(stage, chunk, t, L):
                if stage in ("hi", "lo"):
                    weight(stage, t)
                elif stage == "stats":
                    if L is None and t == 0:
                        eng.wait_ge(s_x0, 16)
                    elif L is None and t == 1:
                        eng.wait_ge(s_xr, 16)
                    elif L is not None:
                        eng.wait_ge(s_x2, x2_adds.peek(L) + 1)
                    elif t >= NT:
                        eng.wait_ge(s_x2, NT + 1)
                    norm_stats(norms_a.next(L), t, 1.0, EPS)
                elif stage == "norm":
                    norm_apply(norms_b.next(L), t)
                elif stage == "att_stats":
                    eng.wait_ge(s_x1, t + 1)
                    norm_stats(norms_a.next(L), t, 1.0 + EPS, EPS * EPS)
                elif stage == "att_norm":
                    norm_apply(norms_b.next(L), t)
                elif stage == "t":
                    eng.wait_ge(s_xhi, t + 1)
                    eng.tensor_tensor(xn_lo[:, :], xt_ps[:, :], xn_hi[:, :].bitcast(F32),
                                      ALU.subtract).then_inc(s_xlo, 1)
                elif stage == "p1":
                    gate_up(t, chunk)
                elif stage == "l1":
                    low(1, t, chunk)
                elif stage in ("p2", "p3"):
                    low(int(stage[1]), t, chunk)
                elif stage == "dt":
                    eng.wait_ge(s_dt, t + 1)
                    xt = x_sb[:, bass.ds(t * TOK, TOK)]
                    eng.tensor_tensor(xt, xt, y_ps[:, :], ALU.add).then_inc(s_x1, 1)
                elif stage == "att_cumsum":
                    eng.wait_ge(s_kw, t + 1)
                    for b in batches():
                        cs = eng.tensor_tensor_scan(csum[:, b], ones[:, :], kw[:, b], 0.0, ALU.mult, ALU.add)
                    cs.then_inc(s_cs, 1)
                elif stage == "att_recip":
                    eng.wait_ge(s_cs, t + 1)
                    b = batches()[chunk]
                    eng.reciprocal(rcsum[:, b], csum[:, b]).then_inc(s_rc, 1)
                elif stage == "att_weight":
                    eng.wait_ge(s_rc, (t + 1) * (TOK // seq))
                    eng.tensor_tensor(wgt[:, :], kw[:, :], rcsum[:, :], ALU.mult).then_inc(s_wg, 1)
                elif stage == "att_weight_keys":
                    eng.wait_ge(s_wg, t + 1)
                    eng.tensor_tensor(wgt_keys[:, :], wgt[:, :], keys[:, :], ALU.mult).then_inc(s_wgk, 1)
                elif stage == "att_pool":
                    eng.wait_ge(s_wgk, t + 2)
                    for b in batches():
                        pl = eng.tensor_tensor_scan(pooled[:, b], ones[:, :], wgt_keys[:, b], 0.0,
                                                    ALU.mult, ALU.add)
                    pl.then_inc(s_pool, 1)
                elif stage == "att_values":
                    eng.wait_ge(s_pool, t + 1)
                    eng.wait_ge(s_x2, t + 1)
                    eng.wait_ge(s_val, t + 1)
                    eng.scalar_tensor_tensor(adelta[:, :], xt_ps[:, :], col("bv"), pooled[:, :],
                                             ALU.add, ALU.mult).then_inc(s_adelta, 1)
                elif stage == "att_dt":
                    x2_adds.next(L)
                    eng.wait_ge(s_at, t + 1)
                    eng.tensor_tensor(x_sb[:, bass.ds(t * TOK + NT * TOK, TOK)], x_sb[:, bass.ds(t * TOK, TOK)],
                                      y_ps[:, :], ALU.add).then_inc(s_x2, 1)

            schedule("DVE", emit, True)
            eng.wait_ge(s_wabs, len(names))
            eng.tensor_reduce(lo_sums[:, :], lo_sum[:, :], AX_X, ALU.add).then_inc(s_wsum, 1)
            eng.wait_ge(s_wsum, 1)
            eng.tensor_scalar(inexact[:, :], lo_sums[:, :], 0.0, None, ALU.is_gt).then_inc(s_inexact, 1)
            eng.wait_ge(s_fps, 1)
            eng.tensor_copy(flag_i[0:1, :], y_ps[0:1, 0:1]).then_inc(s_flag, 1)
            schedule("DVE", emit, False)


def kernel(**inputs):
    import numpy as _np
    import concourse.bacc as _bacc
    from concourse import mybir as _mybir
    from concourse.bass_utils import run_bass_kernel_spmd as _run

    def get(n):
        return _np.asarray(inputs[n])

    X = get("L0_attn_hidden_states")
    nb, seq, D = X.shape
    arrays = {"x": _np.ascontiguousarray(X.reshape(nb * seq, D))}
    for n, src in (("w1t", "L0_ffn_w1_w"), ("w2t", "L0_ffn_w2_w"), ("h1t", "L0_ffn_h1_w"), ("h2t", "L0_ffn_h2_w"),
                   ("w3t", "L0_ffn_w3_w"), ("wkt", "L0_attn_Wk"), ("wkat", "L0_attn_Wka"), ("wvt", "L0_attn_Wv")):
        arrays[n] = _np.ascontiguousarray(get(src).T)
    cols = [get(f"L0_ffn_{n}_s").reshape(-1, P).T for n in ("w1", "w2", "h1", "h2", "w3")]
    cols += [get(f"L0_attn_{n}").reshape(1, P).T for n in ("gamma", "beta", "bk", "bka", "bv")]
    arrays["vecs"] = _np.ascontiguousarray(_np.concatenate(cols, axis=1))

    nc = _bacc.Bacc("TRN2", target_bir_lowering=False, num_devices=1)
    args = [nc.dram_tensor(n, a.shape, _mybir.dt.from_np(a.dtype), kind="ExternalInput").ap()
            for n, a in arrays.items()]
    out = nc.dram_tensor("out", (nb * seq, D), F32, kind="ExternalOutput").ap()
    macaron_block(nc, *args, out, seq)
    r = _run(nc, [arrays], core_ids=[0])
    return r.results[0]["out"].reshape(nb, seq, D)
```

```python
from contextlib import ExitStack

import concourse.bass as bass
from concourse import mybir

P = 128
F32 = mybir.dt.float32
F32R = mybir.dt.float32r
I32 = mybir.dt.int32
ALU = mybir.AluOpType
ACT = mybir.ActivationFunctionType
AX_X = mybir.AxisListType.X

TOK = 512
SUB = TOK // P
ACT_Z = 2
EPS = 1e-5
WARM_UP = 10

VEC = {"s1": (0, 4), "s2": (4, 4), "sh1": (8, 4), "sh2": (12, 4), "s3": (16, 1),
       "gamma": (17, 1), "beta": (18, 1), "bk": (19, 1), "bka": (20, 1), "bv": (21, 1)}
NVEC = 22

START = {
    "PE": (
        "",
        "t p1.0 p1.1 p1.2 p1.3",
    ),
    "ACT": (
        "zwait z abs:w2",
        "t abs:w1 tanh.0 tanh.1 abs:h1 high1.0 tanh.2 abs:w3 tanh.3 abs:h2 high1.1 high1.2 high1.3 zwait z",
    ),
    "DVE": (
        "stats aggr veps hi:w2 lo:w2 hi:w1 norm lo:w1 hi:h1",
        "t hi:h2 gate.0 up.0 hi:w3 gate.1 up.1 lo:h2 low1.0 gate.2 gate.3 stats flag:raise up.2 flag:copy "
        "low1.1 aggr up.3 veps low1.2 low1.3 norm",
    ),
}
ORDER = {
    "PE": (
        "p2.0 p2.1 t p2.2 p1.0 p1.1 p2.3 a:t p1.2 p4 p1.3 a:keys p3.0 p3.1 dt a:logits p3.2 p3.3",
        "t p2.0 p2.1 p1.0 p1.1 p4 p2.2 a:values p2.3 b:t dt p1.2 p1.3 a:dt p3.0 b:keys p3.1 p3.2 p3.3 "
        "b:logits",
        "p4 p2.0 p2.1 t p2.2 p1.0 dt b:values p1.1 p2.3 p1.2 b:dt p3.0 p1.3 p3.1 p3.2 p3.3",
        "p2.0 p2.1 t p2.2 p1.0 p2.3 p1.1 p1.2 p4 p3.0 p3.1 p1.3 p3.2 dt p3.3",
    ),
    "ACT": (
        "gelu2.0 t high2.0 gelu2.1 high2.1 a:zwait gelu2.2 tanh.0 a:z high2.2 tanh.1 gelu2.3 a:t tanh.2 "
        "high1.0 zwait high2.3 high1.1 z tanh.3 high1.2 p4 a:keys gelu3.0 high1.3 high3.0 gelu3.1 a:logits "
        "high3.1 gelu3.2 gelu3.3 high3.2 high3.3",
        "t b:zwait gelu2.0 gelu2.1 b:z high2.0 tanh.0 high2.1 gelu2.2 p4 tanh.1 high2.2 gelu2.3 high1.0 b:t "
        "high1.1 high2.3 tanh.2 tanh.3 b:keys gelu3.0 high1.2 gelu3.1 high3.0 high3.1 high1.3 gelu3.2 "
        "high3.2 zwait gelu3.3 high3.3 b:logits z",
        "gelu2.0 p4 high2.0 gelu2.1 t high2.1 tanh.0 gelu2.2 high2.2 tanh.1 gelu2.3 high1.0 high2.3 high1.1 "
        "tanh.2 gelu3.0 high3.0 tanh.3 gelu3.1 high3.1 high1.2 gelu3.2 high3.2 high1.3 gelu3.3 zwait "
        "high3.3 z",
        "gelu2.0 t gelu2.1 high2.0 high2.1 tanh.0 gelu2.2 high2.2 gelu2.3 high2.3 tanh.1 tanh.2 high1.0 "
        "gelu3.0 zwait high1.1 p4 high3.0 gelu3.1 tanh.3 high1.2 high3.1 gelu3.2 high1.3 high3.2 gelu3.3 z "
        "high3.3",
    ),
    "DVE": (
        "a:stats a:aggr a:veps t low2.0 a:norm stats low2.1 gate.0 up.0 aggr veps gate.1 low2.2 up.1 gate.2 "
        "low1.0 up.2 low2.3 low1.1 gate.3 up.3 low1.2 norm dt low3.0 low1.3 b:stats a:cumsum b:aggr b:veps "
        "low3.1 a:recip.0 low3.2 low3.3",
        "t a:recip.1 a:weight b:norm gate.0 low2.0 a:weight_keys up.0 low2.1 a:pool a:values gate.1 low2.2 "
        "up.1 dt low1.0 low1.1 low2.3 gate.2 up.2 gate.3 a:dt stats up.3 aggr veps low3.0 low3.1 low3.2 "
        "norm low1.2 low3.3 low1.3 b:cumsum b:recip.0",
        "b:recip.1 low2.0 t b:weight low2.1 b:weight_keys gate.0 b:pool dt up.0 gate.1 b:values low2.2 up.1 "
        "low2.3 low1.0 b:dt gate.2 stats up.2 gate.3 low3.0 low1.1 aggr up.3 veps low3.1 low1.2 low1.3 norm "
        "low3.2 low3.3",
        "stats t low2.0 aggr low2.1 gate.0 veps up.0 low2.2 low2.3 gate.1 norm up.1 low1.0 low1.1 gate.2 "
        "up.2 low3.0 gate.3 up.3 low1.2 low3.1 low1.3 dt low3.2 low3.3",
    ),
}
POOL_LOW = ("h1", "w3")
AHEAD = {"stats": 2, "aggr": 2, "veps": 2, "norm": 2, "zwait": 2, "z": 2, "t": 1, "p1": 1, "tanh": 1, "gate": 1,
         "up": 1, "high1": 1, "low1": 1, "p4": -1, "dt": -1}


def macaron_block(nc, x, w1t, w2t, h1t, h2t, w3t, wkt, wkat, wvt, vecs, out, seq):
    ntok, D = x.shape
    HID = w1t.shape[1]
    MC = HID // P
    NT = ntok // TOK
    NB = ntok // P
    SCALE = float(D) ** -0.5
    assert D == P and TOK % seq == 0

    with ExitStack() as ctx:
        def sb(name, shape, dt=F32):
            return ctx.enter_context(nc.sbuf_tensor(name, shape, dt))

        def bank(name):
            return ctx.enter_context(nc.psum_tensor(name, [P, TOK], F32))

        def sem(name):
            return ctx.enter_context(nc.semaphore(name))

        x_sb = sb("x_sb", [P, 2 * NB * P])
        vec = sb("vec", [P, NVEC])
        names = {"w1": (1, HID), "w2": (1, HID), "h1": (MC, HID), "h2": (MC, HID), "w3": (MC, D)}
        raw = {n: sb(f"raw_{n}", [P, k * m]) for n, (k, m) in names.items()}
        whi = {n: sb(f"hi_{n}", [P, k * m], F32R) for n, (k, m) in names.items()}
        wlo = {n: sb(f"lo_{n}", [P, k * m], F32R) for n, (k, m) in names.items()}
        wk = sb("wk", [P, D])
        wka = sb("wka", [P, D])
        wv = sb("wv", [P, D])
        ident = sb("ident", [P, P])
        ones = sb("ones", [P, seq])
        half = sb("half", [P, SUB])
        s1_half = sb("s1_half", [P, MC])
        s12_half = sb("s12_half", [P, MC])
        s3_half = sb("s3_half", [P, 1])
        bka_s = sb("bka_s", [P, 1])
        lo_abs = sb("lo_abs", [P, MC * HID])
        lo_sum = sb("lo_sum", [P, len(names)])
        lo_sums = sb("lo_sums", [P, 1])
        inexact = sb("inexact", [P, 1])
        flag_i = sb("flag_i", [P, 1], I32)
        stats = sb("stats", [P, SUB, 6])
        mv = sb("mv", [P, SUB, 2])
        veps = sb("veps", [P, SUB])
        fence = sb("fence", [P, 1])
        neg_mean = sb("neg_mean", [P, SUB])
        rstd = sb("rstd", [P, SUB])
        nmr = sb("nmr", [P, SUB])
        z = sb("z", [P, TOK])
        xn_hi = sb("xn_hi", [P, TOK], F32R)
        xn_lo = sb("xn_lo", [P, TOK], F32R)
        tanh_b = [sb(f"tanh_{i}", [P, TOK]) for i in range(2)]
        gate_b = [sb(f"gate_{i}", [P, TOK]) for i in range(2)]
        full1 = [sb(f"full1_{i}", [P, TOK]) for i in range(2)]
        full23 = [sb(f"full23_{i}", [P, TOK]) for i in range(2)]
        act_hi = {n: sb(f"act{n}_hi", [P, MC, TOK], F32R) for n in (1, 2, 3)}
        act_lo = {n: sb(f"act{n}_lo", [P, MC, TOK], F32R) for n in (1, 2, 3)}
        delta = sb("delta", [P, TOK])
        adelta = sb("adelta", [P, TOK])
        h_t = sb("h_t", [P, TOK])
        keys = sb("keys", [P, TOK])
        kw = sb("kw", [P, TOK])
        csum = sb("csum", [P, TOK])
        rcsum = sb("rcsum", [P, TOK])
        wgt = sb("wgt", [P, TOK])
        wgt_keys = sb("wgt_keys", [P, TOK])
        pooled = sb("pooled", [P, TOK])

        gate_ps = [bank(f"gate_ps{i}") for i in range(2)]
        up_ps = [bank(f"up_ps{i}") for i in range(2)]
        hid_ps = [bank(f"hid_ps{i}") for i in range(2)]
        y_ps = bank("y_ps")
        xt_ps = bank("xt_ps")

        s_x0, s_xr, s_vec, s_w1, s_w2, s_wh1, s_wh2, s_w3, s_watt, s_out = (
            sem(n) for n in ("s_x0", "s_xr", "s_vec", "s_w1", "s_w2", "s_wh1", "s_wh2", "s_w3", "s_watt", "s_out"))
        s_const = sem("s_const")
        s_small = sem("s_small")
        s_whi = {n: sem(f"s_whi_{n}") for n in names}
        s_wlo = {n: sem(f"s_wlo_{n}") for n in names}
        s_wabs = sem("s_wabs")
        s_wsum = sem("s_wsum")
        s_inexact = sem("s_inexact")
        s_bn, s_mv, s_ve, s_pow, s_z, s_t = (sem(n) for n in ("s_bn", "s_mv", "s_ve", "s_pow", "s_z", "s_t"))
        s_nmr, s_za = sem("s_nmr"), sem("s_za")
        s_xhi, s_xlo = sem("s_xhi"), sem("s_xlo")
        s_fps = sem("s_fps")
        s_flag = sem("s_flag")
        s_p1, s_tanh, s_gate, s_full1 = (sem(n) for n in ("s_p1", "s_tanh", "s_gate", "s_full1"))
        s_p = {n: sem(f"s_p{n}") for n in (2, 3)}
        s_gelu = {n: sem(f"s_gelu{n}") for n in (2, 3)}
        s_hi = {n: sem(f"s_hi{n}") for n in (1, 2, 3)}
        s_lo = {n: sem(f"s_lo{n}") for n in (1, 2, 3)}
        s_p4, s_delta, s_dt, s_x1 = (sem(n) for n in ("s_p4", "s_delta", "s_dt", "s_x1"))
        s_ht, s_key, s_keysb, s_att, s_kw, s_val = (
            sem(n) for n in ("s_ht", "s_key", "s_keysb", "s_att", "s_kw", "s_val"))
        s_cs, s_rc, s_wg, s_wgk, s_pool, s_adelta, s_at, s_x2 = (
            sem(n) for n in ("s_cs", "s_rc", "s_wg", "s_wgk", "s_pool", "s_adelta", "s_at", "s_x2"))

        w_loaded = {"w1": (s_w1, 16), "w2": (s_w2, 16), "h1": (s_wh1, 16), "h2": (s_wh2, 16), "w3": (s_w3, 16)}

        def col(name, m=0):
            return vec[:, VEC[name][0] + m:VEC[name][0] + m + 1]

        def wblk(parts, name, k, m):
            n = names[name][1]
            return parts[name][:, k * n + m * P:k * n + (m + 1) * P]

        def xblk(t, j):
            return x_sb[:, bass.ds(t * TOK + j * P, P)]

        block = ctx.enter_context(nc.Block())

        @block.sync
        def _(eng):
            def xload(t0, t1, s):
                src = x[t0 * TOK:t1 * TOK, :].rearrange("(b p) d -> p b d", p=P)
                dst = x_sb[:, t0 * TOK:t1 * TOK].rearrange("p (b d) -> p b d", d=P)
                eng.dma_start(dst, src).then_inc(s, 16)

            def wload(dst, src, s):
                k = src.shape[0] // P
                eng.dma_start(dst[:, :].rearrange("p (k n) -> p k n", k=k),
                              src.rearrange("(k p) n -> p k n", p=P)).then_inc(s, 16)

            xload(0, 1, s_x0)
            wload(raw["w1"], w1t, s_w1)
            wload(raw["w2"], w2t, s_w2)
            wload(raw["h1"], h1t, s_wh1)
            wload(raw["h2"], h2t, s_wh2)
            wload(raw["w3"], w3t, s_w3)
            xload(1, NT, s_xr)
            for dst, src in ((wk, wkt), (wka, wkat), (wv, wvt)):
                wload(dst, src, s_watt)
            with eng.Fori(0, NT) as t:
                eng.wait_ge(s_x1, t + (NT + 1))
                dst = out[bass.ds(t * TOK, TOK), :].rearrange("(b p) d -> p b d", p=P)
                src = x_sb[:, bass.ds(t * TOK + NT * TOK, TOK)].rearrange("p (b d) -> p b d", d=P)
                eng.dma_start(dst, src).then_inc(s_out, 16)
            eng.wait_ge(s_out, 16 * NT)

        @block.gpsimd
        def _(eng):
            for s in (s_adelta, s_x2, s_wgk, s_za):
                eng.sem_inc(s, 1)
            eng.memset(ident[:, :], 0.0).then_inc(s_const, 1)
            eng.memset(ones[:, :], 1.0).then_inc(s_const, 1)
            eng.memset(half[:, :], -0.5).then_inc(s_const, 1)
            eng.wait_ge(s_const, 3)
            eng.affine_select(out=ident[:, :], in_=ident[:, :], compare_op=ALU.not_equal, fill=1.0,
                              base=0, pattern=[[-1, P]], channel_multiplier=1).then_inc(s_const, 1)

            def norm(n):
                eng.wait_ge(s_ve, n + 1)
                eng.wait_ge(s_za, n + 1)
                eng.tensor_tensor(rstd[:, :], veps[:, :], half[:, :], ALU.pow).then_inc(s_pow, 1)
                eng.wait_ge(s_pow, n + 1)
                eng.tensor_tensor(nmr[:, :], neg_mean[:, :], rstd[:, :], ALU.mult).then_inc(s_nmr, 1)

            norm(0)
            for n in POOL_LOW:
                eng.wait_ge(s_whi[n], 1)
                eng.tensor_tensor(wlo[n][:, :], raw[n][:, :], whi[n][:, :].bitcast(F32),
                                  ALU.subtract).then_inc(s_wlo[n], 1)
            with eng.Fori(1, 3 * NT) as n:
                norm(n)

        GROUP, ATT = 3, 2
        FIRST = 2
        LOOPS = NT // ATT
        assert FIRST + GROUP * LOOPS + 2 == 2 * NT

        def schedule(engine, emit, start):
            def step(i, order, L):
                for item in order.split():
                    which, _, stage = item.rpartition(":")
                    stage, _, chunk = stage.partition(".")
                    chunk = int(chunk) if chunk else None
                    if which in ("hi", "lo", "abs", "flag"):
                        emit(which, None, stage, L)
                    elif which and L is not None:
                        emit("att_" + stage, chunk, ATT * L + "ab".index(which), L)
                    elif not which:
                        t = i + AHEAD.get(stage, 0)
                        if not isinstance(t, int) or 0 <= t < 2 * NT:
                            emit(stage, chunk, t, L)

            eng, orders = {"PE": nc.tensor, "ACT": nc.scalar, "DVE": nc.vector}[engine], ORDER[engine]
            if start:
                step(-2, START[engine][0], None)
                step(-1, START[engine][1], None)
                return
            for i in range(0, FIRST):
                step(i, orders[GROUP], None)
            with eng.Fori(0, LOOPS) as L:
                for s in range(GROUP):
                    step(GROUP * L + (FIRST + s), orders[s], L)
            for i in range(2 * NT - 2, 2 * NT + 1):
                step(i, orders[GROUP], None)

        class Uses:
            def __init__(self, start, per_loop):
                self.n, self.per_loop, self.loop_base = start, per_loop, None

            def peek(self, L):
                if L is not None and self.loop_base is None:
                    self.loop_base = self.n
                if L is None and self.loop_base is not None:
                    assert self.n == self.loop_base + self.per_loop
                    self.n, self.loop_base = self.n + (LOOPS - 1) * self.per_loop, None
                return self.n if L is None else L * self.per_loop + self.n

            def next(self, L):
                n = self.peek(L)
                self.n += 1
                return n

        @block.tensor
        def _(eng):
            def products(ps, parts, done, general):
                seq_ = []
                for name, k, m, hi, lo in parts:
                    for a, ready in (hi, lo):
                        seq_.append((wblk(whi, name, k, m), a, ready))
                        if general:
                            seq_.append((wblk(wlo, name, k, m), a, None))
                for n, (w, a, ready) in enumerate(seq_):
                    if ready is not None:
                        eng.wait_ge(*ready)
                    mm = eng.matmul(ps, w, a, start=(n == 0), stop=(n == len(seq_) - 1))
                if done is not None:
                    mm.then_inc(done, 1)

            def layer(n, T, k, wait):
                c = MC * T + k + 1
                return ((act_hi[n][:, k, :], (s_hi[n], c) if wait else None),
                        (act_lo[n][:, k, :], (s_lo[n], c) if wait else None))

            def transpose4(dst, src, done):
                for j in range(SUB):
                    mm = eng.transpose(dst[:, j * P:(j + 1) * P], src[:, j * P:(j + 1) * P], ident[:, :])
                mm.then_inc(done, 1)

            def p1(T, m, general):
                c = MC * T + m
                if isinstance(T, int) and c == 0:
                    for n in ("w1", "w2"):
                        eng.wait_ge(s_whi[n], 1)
                        eng.wait_ge(s_wlo[n], 1)
                if not (isinstance(T, int) and c < 2):
                    eng.wait_ge(s_full1, c - 1)
                hi, lo = (xn_hi[:, :], (s_xhi, T + 1)), (xn_lo[:, :], (s_xlo, T + 1))
                if m > 0:
                    hi, lo = (hi[0], None), (lo[0], None)
                products(gate_ps[m % 2][:, :], [("w1", 0, m, hi, lo)], None, general)
                products(up_ps[m % 2][:, :], [("w2", 0, m, (hi[0], None), (lo[0], None))], s_p1, general)

            def p23(n, T, m, general):
                prev, w = (1, "h1") if n == 2 else (2, "h2")
                if n == 2 and m < 2:
                    if not (isinstance(T, int) and T == 0):
                        eng.wait_ge(s_gelu[3], MC * T - MC + m + 3)
                elif n == 3 and m < 2:
                    eng.wait_ge(s_gelu[2], MC * T + m + 3)
                else:
                    eng.wait_ge(s_gelu[n], MC * T + m - 1)
                products(hid_ps[m % 2][:, :],
                         [(w, k, m, *layer(prev, T, k, wait=(m == 0))) for k in range(MC)],
                         s_p[n], general)

            def stages(general, transposed, xt_reader):
                norms = Uses(transposed, GROUP + ATT)
                last = {"xt": xt_reader, "y": [(s_flag, 1)], "inside": False}

                def free(bank, reader):
                    for s, n in last[bank]:
                        eng.wait_ge(s, n)
                    last[bank] = [reader]

                def emit(stage, chunk, t, L):
                    if L is not None and not last["inside"]:
                        last.update(xt=[(s_xlo, GROUP * L + FIRST), (s_adelta, ATT * L + 1)],
                                    y=[(s_x1, GROUP * L + (FIRST - 1)), (s_x2, ATT * L + 1)], inside=True)
                    if L is None and last["inside"]:
                        last.update(xt=[(s_xlo, 2 * NT - 1), (s_adelta, NT + 1)],
                                    y=[(s_x1, 2 * NT - 3), (s_x2, NT + 1)], inside=False)
                    if stage == "p1":
                        p1(t, chunk, general)
                    elif stage in ("p2", "p3"):
                        p23(int(stage[1]), t, chunk, general)
                    elif stage in ("t", "att_t"):
                        n = norms.next(L)
                        eng.wait_ge(s_z, n + 1)
                        eng.wait_ge(s_za, n + 2)
                        free("xt", (s_xlo if stage == "t" else s_ht, t + 1))
                        transpose4(xt_ps, z, s_t)
                    elif stage == "p4":
                        free("y", (s_delta, t + 1))
                        products(y_ps[:, :], [("w3", k, 0, *layer(3, t, k, wait=True)) for k in range(MC)],
                                 s_p4, general)
                    elif stage == "dt":
                        free("y", (s_x1, t + 1))
                        transpose4(y_ps, delta, s_dt)
                    elif stage == "att_keys":
                        free("xt", (s_keysb, t + 1))
                        eng.wait_ge(s_watt, 48)
                        eng.matmul(xt_ps[:, :], wk[:, :], h_t[:, :], start=True, stop=True).then_inc(s_key, 1)
                    elif stage == "att_logits":
                        free("xt", (s_kw, t + 1))
                        eng.matmul(xt_ps[:, :], wka[:, :], keys[:, :], start=True, stop=True).then_inc(s_att, 1)
                    elif stage == "att_values":
                        free("xt", (s_adelta, t + 2))
                        eng.matmul(xt_ps[:, :], wv[:, :], h_t[:, :], start=True, stop=True).then_inc(s_val, 1)
                    elif stage == "att_dt":
                        eng.wait_ge(s_adelta, t + 2)
                        free("y", (s_x2, t + 2))
                        transpose4(y_ps, adelta, s_at)
                return emit

            eng.wait_ge(s_const, 4)
            for _ in range(WARM_UP):
                eng.matmul(y_ps[0:1, 0:seq], ones[:, 0:1], ones[:, :], start=True, stop=True)
            schedule("PE", stages(True, 0, []), True)
            eng.wait_ge(s_inexact, 1)
            eng.matmul(y_ps[0:1, 0:1], inexact[:, 0:1], ones[:, 0:1], start=True, stop=True).then_inc(s_fps, 1)
            with eng.register("flag") as flag:
                eng.wait_ge(s_flag, 1)
                eng.reg_load(flag, flag_i[0:1, 0:1])
                with eng.If_ne(flag, 0):
                    schedule("PE", stages(True, 1, [(s_xlo, 1)]), False)
                with eng.Else():
                    schedule("PE", stages(False, 1, [(s_xlo, 1)]), False)

        @block.scalar
        def _(eng):
            eng.dma_start(vec[:, :], vecs).then_inc(s_vec, 16)

            abs_order = [i[4:] for i in " ".join(START["ACT"]).split() if i.startswith("abs:")]

            def weight(what, n):
                if what == "hi":
                    eng.wait_ge(*w_loaded[n])
                    eng.activation(whi[n][:, :], raw[n][:, :], ACT.Copy).then_inc(s_whi[n], 1)
                else:
                    q = abs_order.index(n)
                    eng.wait_ge(s_wlo[n], 1)
                    if q > 0:
                        eng.wait_ge(s_wabs, q)
                    eng.activation(lo_abs[:, 0:wlo[n].shape[1]], wlo[n][:, :].bitcast(F32), ACT.Abs,
                                   accum_out=lo_sum[:, q:q + 1]).then_inc(s_wabs, 1)

            def tanh(T, m):
                c = MC * T + m
                if isinstance(T, int) and c == 0:
                    eng.wait_ge(s_small, 4)
                eng.wait_ge(s_p1, c + 1)
                if not (isinstance(T, int) and c < 2):
                    eng.wait_ge(s_gate, c - 1)
                eng.activation(tanh_b[m % 2][:, :], gate_ps[m % 2][:, :], ACT.Tanh,
                               scale=s1_half[:, m:m + 1]).then_inc(s_tanh, 1)

            def high1(T, m):
                eng.wait_ge(s_full1, MC * T + m + 1)
                eng.activation(act_hi[1][:, m, :], full1[m % 2][:, :], ACT.Copy).then_inc(s_hi[1], 1)

            def gelu(n, T, m):
                eng.wait_ge(s_p[n], MC * T + m + 1)
                if n == 2 and m < 2:
                    if not (isinstance(T, int) and T == 0):
                        eng.wait_ge(s_lo[3], MC * T - MC + m + 3)
                elif n == 3 and m < 2:
                    eng.wait_ge(s_lo[2], MC * T + m + 3)
                else:
                    eng.wait_ge(s_lo[n], MC * T + m - 1)
                eng.activation(full23[m % 2][:, :], hid_ps[m % 2][:, :], ACT.Gelu,
                               scale=col("sh1" if n == 2 else "sh2", m)).then_inc(s_gelu[n], 1)

            def high23(n, T, m):
                eng.wait_ge(s_gelu[n], MC * T + m + 1)
                eng.activation(act_hi[n][:, m, :], full23[m % 2][:, :], ACT.Copy).then_inc(s_hi[n], 1)

            def z_blocks(t):
                for j in range(ACT_Z):
                    zz = eng.activation(z[:, j * P:(j + 1) * P], xblk(t, j), ACT.Identity, bias=nmr[:, j:j + 1],
                                        scale=rstd[:, j:j + 1])
                zz.then_inc(s_za, 1)

            norms, z_norms = Uses(0, GROUP + ATT), Uses(0, GROUP + ATT)

            def emit(stage, chunk, t, L):
                if stage in ("hi", "abs"):
                    weight(stage, t)
                elif stage == "tanh":
                    tanh(t, chunk)
                elif stage == "high1":
                    high1(t, chunk)
                elif stage in ("zwait", "att_zwait"):
                    n = z_norms.next(L)
                    eng.wait_ge(s_nmr, n + 1)
                    if not isinstance(n, int) or n > 0:
                        eng.wait_ge(s_t, n)
                elif stage in ("z", "att_z"):
                    z_blocks(t)
                elif stage in ("gelu2", "gelu3"):
                    gelu(int(stage[-1]), t, chunk)
                elif stage in ("high2", "high3"):
                    high23(int(stage[-1]), t, chunk)
                elif stage == "p4":
                    eng.wait_ge(s_p4, t + 1)
                    eng.activation(delta[:, :], y_ps[:, :], ACT.Copy, scale=s3_half[:, 0:1]).then_inc(s_delta, 1)
                elif stage == "t":
                    eng.wait_ge(s_t, norms.next(L) + 1)
                    eng.activation(xn_hi[:, :], xt_ps[:, :], ACT.Copy).then_inc(s_xhi, 1)
                elif stage == "att_t":
                    eng.wait_ge(s_t, norms.next(L) + 1)
                    eng.activation(h_t[:, :], xt_ps[:, :], ACT.Identity, bias=col("beta"),
                                   scale=col("gamma")).then_inc(s_ht, 1)
                elif stage == "att_keys":
                    eng.wait_ge(s_key, t + 1)
                    eng.wait_ge(s_wgk, t + 1)
                    eng.activation(keys[:, :], xt_ps[:, :], ACT.Identity, bias=col("bk")).then_inc(s_keysb, 1)
                elif stage == "att_logits":
                    eng.wait_ge(s_att, t + 1)
                    eng.activation(kw[:, :], xt_ps[:, :], ACT.Exp, bias=bka_s[:, 0:1],
                                   scale=SCALE).then_inc(s_kw, 1)

            schedule("ACT", emit, True)
            schedule("ACT", emit, False)

        @block.vector
        def _(eng):
            eng.wait_ge(s_vec, 16)
            eng.tensor_scalar(s1_half[:, :], vec[:, 0:MC], 0.5, None, ALU.mult).then_inc(s_small, 1)
            eng.tensor_scalar(s3_half[:, :], col("s3"), 0.5, None, ALU.mult).then_inc(s_small, 1)
            eng.tensor_scalar(bka_s[:, :], col("bka"), SCALE, None, ALU.mult).then_inc(s_small, 1)
            eng.wait_ge(s_small, 3)
            eng.tensor_tensor(s12_half[:, :], s1_half[:, :], vec[:, 4:4 + MC], ALU.mult).then_inc(s_small, 1)

            def weight(what, n):
                if what == "hi":
                    eng.wait_ge(*w_loaded[n])
                    eng.tensor_copy(whi[n][:, :], raw[n][:, :]).then_inc(s_whi[n], 1)
                else:
                    eng.wait_ge(*w_loaded[n])
                    eng.wait_ge(s_whi[n], 1)
                    eng.tensor_tensor(wlo[n][:, :], raw[n][:, :], whi[n][:, :].bitcast(F32),
                                      ALU.subtract).then_inc(s_wlo[n], 1)

            def raise_flag():
                eng.wait_ge(s_wabs, len(names))
                eng.tensor_reduce(lo_sums[:, :], lo_sum[:, :], AX_X, ALU.add).then_inc(s_wsum, 1)
                eng.wait_ge(s_wsum, 1)
                eng.tensor_scalar(inexact[:, :], lo_sums[:, :], 0.0, None, ALU.is_gt).then_inc(s_inexact, 1)

            def copy_flag():
                eng.wait_ge(s_fps, 1)
                eng.tensor_copy(flag_i[0:1, :], y_ps[0:1, 0:1]).then_inc(s_flag, 1)

            def norm_stats(t):
                for j in range(SUB):
                    eng.bn_stats(stats[:, j, :], xblk(t, j)).then_inc(s_bn, 1)

            def norm_aggr(n):
                eng.wait_ge(s_bn, SUB * n + SUB)
                eng.memset(fence[:, :], 0.0)
                for j in range(SUB):
                    eng.bn_aggr(mv[:, j, :], stats[:, j, :]).then_inc(s_mv, 1)

            def norm_veps(n, a, b):
                eng.wait_ge(s_mv, SUB * n + SUB)
                eng.tensor_scalar(neg_mean[:, :], mv[:, :, 0], -1.0, None, ALU.mult)
                eng.tensor_scalar(veps[:, :], mv[:, :, 1], a, b, ALU.mult, ALU.add).then_inc(s_ve, 1)

            def norm_apply(n, t):
                eng.wait_ge(s_nmr, n + 1)
                if not isinstance(n, int) or n > 0:
                    eng.wait_ge(s_t, n)
                for j in range(ACT_Z, SUB):
                    zz = eng.tensor_scalar(z[:, j * P:(j + 1) * P], xblk(t, j), mv[:, j, 0:1], rstd[:, j:j + 1],
                                           ALU.subtract, ALU.mult)
                zz.then_inc(s_z, 1)

            def gate(T, m):
                c = MC * T + m
                eng.wait_ge(s_tanh, c + 1)
                if not (isinstance(T, int) and c < 2):
                    eng.wait_ge(s_full1, c - 1)
                eng.scalar_tensor_tensor(gate_b[m % 2][:, :], tanh_b[m % 2][:, :], 1.0, gate_ps[m % 2][:, :],
                                         ALU.add, ALU.mult).then_inc(s_gate, 1)

            def up(T, m):
                c = MC * T + m
                eng.wait_ge(s_gate, c + 1)
                if not (isinstance(T, int) and c < 2):
                    eng.wait_ge(s_lo[1], c - 1)
                eng.scalar_tensor_tensor(full1[m % 2][:, :], up_ps[m % 2][:, :], s12_half[:, m:m + 1],
                                         gate_b[m % 2][:, :], ALU.mult, ALU.mult).then_inc(s_full1, 1)

            def low(n, T, m):
                eng.wait_ge(s_hi[n], MC * T + m + 1)
                full = full1 if n == 1 else full23
                eng.tensor_tensor(act_lo[n][:, m, :], full[m % 2][:, :], act_hi[n][:, m, :].bitcast(F32),
                                  ALU.subtract).then_inc(s_lo[n], 1)

            def batches():
                return [slice(b * seq, (b + 1) * seq) for b in range(TOK // seq)]

            norms = {stage: Uses(0, GROUP + ATT) for stage in ("aggr", "veps", "norm")}
            x2_adds = Uses(0, ATT)

            def emit(stage, chunk, t, L):
                if stage in ("hi", "lo"):
                    weight(stage, t)
                elif stage == "flag":
                    (raise_flag if t == "raise" else copy_flag)()
                elif stage == "stats":
                    if L is None and t == 0:
                        eng.wait_ge(s_x0, 16)
                    elif L is None and t == 1:
                        eng.wait_ge(s_xr, 16)
                    elif L is not None:
                        eng.wait_ge(s_x2, x2_adds.peek(L) + 1)
                    elif t >= NT:
                        eng.wait_ge(s_x2, NT + 1)
                    norm_stats(t)
                elif stage == "att_stats":
                    eng.wait_ge(s_x1, t + 1)
                    norm_stats(t)
                elif stage in ("aggr", "att_aggr"):
                    norm_aggr(norms["aggr"].next(L))
                elif stage == "veps":
                    norm_veps(norms["veps"].next(L), 1.0, EPS)
                elif stage == "att_veps":
                    norm_veps(norms["veps"].next(L), 1.0 + EPS, EPS * EPS)
                elif stage in ("norm", "att_norm"):
                    norm_apply(norms["norm"].next(L), t)
                elif stage == "t":
                    eng.wait_ge(s_xhi, t + 1)
                    eng.tensor_tensor(xn_lo[:, :], xt_ps[:, :], xn_hi[:, :].bitcast(F32),
                                      ALU.subtract).then_inc(s_xlo, 1)
                elif stage == "gate":
                    gate(t, chunk)
                elif stage == "up":
                    up(t, chunk)
                elif stage in ("low1", "low2", "low3"):
                    low(int(stage[-1]), t, chunk)
                elif stage == "dt":
                    eng.wait_ge(s_dt, t + 1)
                    xt = x_sb[:, bass.ds(t * TOK, TOK)]
                    eng.tensor_tensor(xt, xt, y_ps[:, :], ALU.add).then_inc(s_x1, 1)
                elif stage == "att_cumsum":
                    eng.wait_ge(s_kw, t + 1)
                    for b in batches():
                        cs = eng.tensor_tensor_scan(csum[:, b], ones[:, :], kw[:, b], 0.0, ALU.mult, ALU.add)
                    cs.then_inc(s_cs, 1)
                elif stage == "att_recip":
                    eng.wait_ge(s_cs, t + 1)
                    b = batches()[chunk]
                    eng.reciprocal(rcsum[:, b], csum[:, b]).then_inc(s_rc, 1)
                elif stage == "att_weight":
                    eng.wait_ge(s_rc, (t + 1) * (TOK // seq))
                    eng.tensor_tensor(wgt[:, :], kw[:, :], rcsum[:, :], ALU.mult).then_inc(s_wg, 1)
                elif stage == "att_weight_keys":
                    eng.wait_ge(s_wg, t + 1)
                    eng.tensor_tensor(wgt_keys[:, :], wgt[:, :], keys[:, :], ALU.mult).then_inc(s_wgk, 1)
                elif stage == "att_pool":
                    eng.wait_ge(s_wgk, t + 2)
                    for b in batches():
                        pl = eng.tensor_tensor_scan(pooled[:, b], ones[:, :], wgt_keys[:, b], 0.0,
                                                    ALU.mult, ALU.add)
                    pl.then_inc(s_pool, 1)
                elif stage == "att_values":
                    eng.wait_ge(s_pool, t + 1)
                    eng.wait_ge(s_x2, t + 1)
                    eng.wait_ge(s_val, t + 1)
                    eng.scalar_tensor_tensor(adelta[:, :], xt_ps[:, :], col("bv"), pooled[:, :],
                                             ALU.add, ALU.mult).then_inc(s_adelta, 1)
                elif stage == "att_dt":
                    x2_adds.next(L)
                    eng.wait_ge(s_at, t + 1)
                    eng.tensor_tensor(x_sb[:, bass.ds(t * TOK + NT * TOK, TOK)], x_sb[:, bass.ds(t * TOK, TOK)],
                                      y_ps[:, :], ALU.add).then_inc(s_x2, 1)

            schedule("DVE", emit, True)
            schedule("DVE", emit, False)


def kernel(**inputs):
    import numpy as _np
    import concourse.bacc as _bacc
    from concourse import mybir as _mybir
    from concourse.bass_utils import run_bass_kernel_spmd as _run

    def get(n):
        return _np.asarray(inputs[n])

    X = get("L0_attn_hidden_states")
    nb, seq, D = X.shape
    arrays = {"x": _np.ascontiguousarray(X.reshape(nb * seq, D))}
    for n, src in (("w1t", "L0_ffn_w1_w"), ("w2t", "L0_ffn_w2_w"), ("h1t", "L0_ffn_h1_w"), ("h2t", "L0_ffn_h2_w"),
                   ("w3t", "L0_ffn_w3_w"), ("wkt", "L0_attn_Wk"), ("wkat", "L0_attn_Wka"), ("wvt", "L0_attn_Wv")):
        arrays[n] = _np.ascontiguousarray(get(src).T)
    cols = [get(f"L0_ffn_{n}_s").reshape(-1, P).T for n in ("w1", "w2", "h1", "h2", "w3")]
    cols += [get(f"L0_attn_{n}").reshape(1, P).T for n in ("gamma", "beta", "bk", "bka", "bv")]
    arrays["vecs"] = _np.ascontiguousarray(_np.concatenate(cols, axis=1))

    nc = _bacc.Bacc("TRN2", target_bir_lowering=False, num_devices=1)
    args = [nc.dram_tensor(n, a.shape, _mybir.dt.from_np(a.dtype), kind="ExternalInput").ap()
            for n, a in arrays.items()]
    out = nc.dram_tensor("out", (nb * seq, D), F32, kind="ExternalOutput").ap()
    macaron_block(nc, *args, out, seq)
    r = _run(nc, [arrays], core_ids=[0])
    return r.results[0]["out"].reshape(nb, seq, D)
```
